# Optimizing a Trainium2 kernel written in Bass

```python
import numpy as np
import jax
import jax.numpy as jnp

def _softmax(x, axis=-1):
    return jax.nn.softmax(x, axis=axis)

def _gelu(x):
    return jax.nn.gelu(x, approximate=True)

def _silu(x):
    return jax.nn.silu(x)

def _sigmoid(x):
    return jax.nn.sigmoid(x)

def _layernorm(x, axis=-1, eps=1e-05):
    m = jnp.mean(x, axis=axis, keepdims=True)
    v = jnp.var(x, axis=axis, keepdims=True)
    return (x - m) / jnp.sqrt(v + eps)

def _scatter_add(tgt, idx, src, axis=0):
    return tgt.at[idx].add(src)

def _segment_sum(src, seg, n):
    return jax.ops.segment_sum(src, seg, n)
kernel_name = 'mk_flamingo_gated_d1_seqx_r8_a8dce2'

def setup_inputs(seed: int=0):
    np.random.seed(seed)
    _w = jnp.asarray

    def _rec_inputs():
        import jax
        import jax.numpy as jnp
        _rk = jax.random.key(seed)
        x = -0.0003929 + 0.9999 * jax.random.normal(jax.random.fold_in(_rk, 1), (8, 128, 512), jnp.float32)
        _lenS = 128 - jax.random.randint(jax.random.fold_in(_rk, 7), (8,), 0, max(1, 128 // 4) + 1, jnp.int32)
        _lenS2 = 128 - jax.random.randint(jax.random.fold_in(_rk, 8), (8,), 0, max(1, 128 // 4) + 1, jnp.int32)
        _ctx_4096P = jax.random.normal(jax.random.fold_in(_rk, 11), (8, 16, 512), jnp.float32)
        _ctx_4096c = jax.random.dirichlet(jax.random.fold_in(_rk, 511), 0.3 * jnp.ones((16,), jnp.float32), (8, 128))
        _ctx_4096t = jnp.einsum('bsk,bkd->bsd', _ctx_4096c, _ctx_4096P)
        _ctx_4096t = _ctx_4096t * jax.lax.rsqrt(jnp.mean(jnp.square(_ctx_4096t)) + 1e-12) * 0.953939
        ctx_4096 = 2.81802e-05 + 1.00001 * (_ctx_4096t + 0.3 * jax.random.normal(jax.random.fold_in(_rk, 611), (8, 128, 512), jnp.float32))
        _g = jax.random.normal(jax.random.fold_in(_rk, 9001), (2, 1), jnp.float32)
        _g = jnp.sign(_g) * jnp.maximum(jnp.abs(_g), 1.0) + (_g == 0) * 1.0
        g_xattn = _g[0]
        g_ffn = _g[1]
        return (x, ctx_4096, g_xattn, g_ffn)
    x, ctx_4096, g_xattn, g_ffn = _rec_inputs()

    def _L0_xattn_setup():
        import jax, jax.numpy as jnp
        import numpy as np
        EMBED = 512
        HEADS = 32
        GROUP = 4
        KV_HEADS = HEADS // GROUP
        HEAD_DIM = EMBED // HEADS
        B, S = (2, 256)
        key = jax.random.key(seed)
        ks = jax.random.split(key, 7)
        scale = 0.02
        return {'queries': jax.random.normal(ks[0], (B, S, EMBED), dtype=jnp.float32), 'keys': jax.random.normal(ks[1], (B, S, EMBED), dtype=jnp.float32), 'values': jax.random.normal(ks[2], (B, S, EMBED), dtype=jnp.float32), 'Wq': jax.random.normal(ks[3], (EMBED, EMBED), dtype=jnp.float32) * scale, 'Wk': jax.random.normal(ks[4], (EMBED, KV_HEADS * HEAD_DIM), dtype=jnp.float32) * scale, 'Wv': jax.random.normal(ks[5], (EMBED, KV_HEADS * HEAD_DIM), dtype=jnp.float32) * scale, 'Wo': jax.random.normal(ks[6], (EMBED, EMBED), dtype=jnp.float32) * scale}
    _L0_xattn_all = _L0_xattn_setup()
    _L0_xattn_in = {k: v for k, v in _L0_xattn_all.items() if k in ('Wq', 'Wk', 'Wv', 'Wo')}
    del _L0_xattn_all

    def _L0_ffn_setup():
        import jax, jax.numpy as jnp
        import numpy as np
        HID, INT, LAT, NE, K = (512, 1024, 256, 8, 2)
        LN_EPS = 1e-05

        def _layernorm(x, gamma, beta):
            mu = jnp.mean(x, axis=-1, keepdims=True)
            var = jnp.var(x, axis=-1, keepdims=True)
            return (x - mu) * jax.lax.rsqrt(var + LN_EPS) * gamma + beta
        key = jax.random.key(seed)
        ks = jax.random.split(key, 8)
        s = lambda d: 1.0 / np.sqrt(d)
        return {'hidden_states': jax.random.normal(ks[0], (4, 256, HID), jnp.float32), 'gate_w': jax.random.normal(ks[1], (HID, NE), jnp.float32) * s(HID), 'up_w': jax.random.normal(ks[2], (HID, INT), jnp.float32) * s(HID), 'down_w': jax.random.normal(ks[3], (INT, HID), jnp.float32) * s(INT), 'fc1_w': jax.random.normal(ks[4], (HID, LAT), jnp.float32) * s(HID), 'fc2_w': jax.random.normal(ks[5], (LAT, HID), jnp.float32) * s(LAT), 'expert_w': jax.random.normal(ks[6], (LAT, LAT), jnp.float32), 'ln_gamma': jnp.ones((HID,), jnp.float32), 'ln_beta': jnp.zeros((HID,), jnp.float32)}
    _L0_ffn_all = _L0_ffn_setup()
    _L0_ffn_in = {k: v for k, v in _L0_ffn_all.items() if k in ('gate_w', 'up_w', 'down_w', 'fc1_w', 'fc2_w', 'expert_w', 'ln_gamma', 'ln_beta')}
    del _L0_ffn_all
    return {'x': x, 'ctx_4096': ctx_4096, 'g_xattn': g_xattn, 'g_ffn': g_ffn, 'L0_xattn_Wq': _L0_xattn_in['Wq'], 'L0_xattn_Wk': _L0_xattn_in['Wk'], 'L0_xattn_Wv': _L0_xattn_in['Wv'], 'L0_xattn_Wo': _L0_xattn_in['Wo'], 'L0_ffn_gate_w': _L0_ffn_in['gate_w'], 'L0_ffn_up_w': _L0_ffn_in['up_w'], 'L0_ffn_down_w': _L0_ffn_in['down_w'], 'L0_ffn_fc1_w': _L0_ffn_in['fc1_w'], 'L0_ffn_fc2_w': _L0_ffn_in['fc2_w'], 'L0_ffn_expert_w': _L0_ffn_in['expert_w'], 'L0_ffn_ln_gamma': _L0_ffn_in['ln_gamma'], 'L0_ffn_ln_beta': _L0_ffn_in['ln_beta']}

def reference(x, ctx_4096, g_xattn, g_ffn, L0_xattn_Wq, L0_xattn_Wk, L0_xattn_Wv, L0_xattn_Wo, L0_ffn_gate_w, L0_ffn_up_w, L0_ffn_down_w, L0_ffn_fc1_w, L0_ffn_fc2_w, L0_ffn_expert_w, L0_ffn_ln_gamma, L0_ffn_ln_beta):
    import jax
    import jax.numpy as jnp

    def _L0_xattn_ref(queries, keys, values, Wq, Wk, Wv, Wo):
        import jax, jax.numpy as jnp
        import numpy as np
        EMBED = 512
        HEADS = 32
        GROUP = 4
        KV_HEADS = HEADS // GROUP
        HEAD_DIM = EMBED // HEADS
        B, S = (2, 256)
        b, s, _ = queries.shape
        q = (queries @ Wq).reshape(b, s, KV_HEADS, GROUP, HEAD_DIM)
        k = (keys @ Wk).reshape(b, s, KV_HEADS, HEAD_DIM)
        v = (values @ Wv).reshape(b, s, KV_HEADS, HEAD_DIM)
        scale = 1.0 / jnp.sqrt(jnp.asarray(HEAD_DIM, dtype=q.dtype))
        scores = jnp.einsum('bqhgd,bkhd->bhgqk', q, k) * scale
        attn = jax.nn.softmax(scores, axis=-1)
        out = jnp.einsum('bhgqk,bkhd->bqhgd', attn, v)
        out = out.reshape(b, s, EMBED)
        return out @ Wo

    def _L0_ffn_ref(hidden_states, gate_w, up_w, down_w, fc1_w, fc2_w, expert_w, ln_gamma, ln_beta):
        import jax, jax.numpy as jnp
        import numpy as np
        HID, INT, LAT, NE, K = (512, 1024, 256, 8, 2)
        LN_EPS = 1e-05

        def _layernorm(x, gamma, beta):
            mu = jnp.mean(x, axis=-1, keepdims=True)
            var = jnp.var(x, axis=-1, keepdims=True)
            return (x - mu) * jax.lax.rsqrt(var + LN_EPS) * gamma + beta
        logits = jnp.einsum('bsh,he->bse', hidden_states, gate_w)
        routing_weights, selected_experts = jax.lax.top_k(logits, K)
        h = jax.nn.relu(jnp.einsum('bsh,hi->bsi', hidden_states, up_w)) ** 2
        shared_out = jnp.einsum('bsi,ih->bsh', h, down_w)
        x_latent = jnp.einsum('bsh,hl->bsl', hidden_states, fc1_w)
        expert_out = jnp.einsum('bsl,lm->bsm', x_latent, expert_w)
        moe_out = expert_out * jnp.sum(routing_weights, axis=-1, keepdims=True)
        routed_out = jnp.einsum('bsl,lh->bsh', moe_out, fc2_w)
        return _layernorm(shared_out + routed_out, ln_gamma, ln_beta)
    x = x + jnp.tanh(g_xattn[0]) * _L0_xattn_ref(_layernorm(x, axis=-1), ctx_4096, ctx_4096, L0_xattn_Wq, L0_xattn_Wk, L0_xattn_Wv, L0_xattn_Wo)
    x = x + jnp.tanh(g_ffn[0]) * _L0_ffn_ref(_layernorm(x, axis=-1), L0_ffn_gate_w, L0_ffn_up_w, L0_ffn_down_w, L0_ffn_fc1_w, L0_ffn_fc2_w, L0_ffn_expert_w, L0_ffn_ln_gamma, L0_ffn_ln_beta)
    return x

_drawn_inputs = setup_inputs


def setup_inputs(seed=0):
    import zlib

    import numpy as np

    out = dict(_drawn_inputs(seed))
    spreads = {'L0_ffn_ln_gamma': (1.0, 0.2), 'L0_ffn_ln_beta': (0.0, 0.1)}
    factors = {'L0_xattn_Wq': 6.784, 'L0_xattn_Wk': 7.672}
    for name, (base, spread) in spreads.items():
        noise = np.random.default_rng([zlib.crc32(name.encode()), seed]).standard_normal(out[name].shape)
        drawn = base * np.exp(spread * noise) if base else spread * noise
        out[name] = jnp.asarray(drawn.astype(out[name].dtype))
    for name, factor in factors.items():
        out[name] = (out[name] * factor).astype(out[name].dtype)
    return out
```

```python
from contextlib import ExitStack

import concourse.bass as bass
from concourse import mybir

FP32 = mybir.dt.float32
FP32R = mybir.dt.float32r
ALU = mybir.AluOpType
ACT = mybir.ActivationFunctionType
AX = mybir.AxisListType

P = 128
NSEQ = 8
SEQ = 128
D = 512
KT = D // P
HEADS, KV, HD = 32, 8, 16
GROUP = HEADS // KV
NPAIR = HEADS // 2
PAIRS = NSEQ // 2
T = 2 * SEQ
KVD = KV * HD
INT, LAT, NE = 1024, 256, 8
MT = INT // P
LT = LAT // P
STACK = 3 * 2 * HD
MAXROWS = 4
OWN2 = 7
SCALE = float(HD) ** -0.5
EPS = 1e-5


class Fill:

    def __init__(self, number, loop=0):
        self.bank, self.before, self.loop = number % 2, number // 2, loop

    def full(self):
        return self.before + 1 + self.loop

    def earlier(self):
        return self.before + self.loop


FIRST = ["xT0", "xT1", "cT0", "cT1", "q0", "q1", "k", "K0", "K1", "K2", "K3", "V", "mT0"]
BODY = ["xT0", "xT1", "mT1", "cT0", "cT1", "q0", "q1", "k", "K0", "K1", "K2", "K3", "V", "o0", "mT0", "o1"]
LAST = ["mT1", "eT", "ef0", "ef1", "o0", "o1"]
SPLIT = ["xT0", "xT1", "cT0", "cT1", "q0", "q1", "k"]
WEIGH_AFTER = {5: 0, 8: 1, 12: 2}


def fill_first(name):
    return Fill(FIRST.index(name))


def fill_body(name, i):
    return Fill(len(FIRST) + BODY.index(name), i * (len(BODY) // 2))


def fill_last(name):
    return Fill(len(FIRST) + len(BODY) * (PAIRS - 1) + LAST.index(name))


def flamingo_block(nc, x, ctx, g_attn, g_ffn, Wq, Wk, Wv, Wo, gate_w, up_w, down_w, fc1_w, fc2_w,
                   expert_w, gamma, beta, out):
    stack = ExitStack()
    with stack:
        def sb(name, shape, dt=FP32):
            return stack.enter_context(nc.sbuf_tensor(name, shape, dt))

        def sem(name):
            return stack.enter_context(nc.semaphore(name))

        store = sb("store", [P, 28736], FP32R)
        taken = [0]

        def part(cols, at=None):
            at = taken[0] if at is None else at
            taken[0] = max(taken[0], at + cols)
            return at

        def view(at, *dims):
            n = 1
            for d in dims:
                n *= d
            v = store[:, at:at + n]
            names = "abcde"[:len(dims)]
            if len(dims) > 1:
                v = v.rearrange(f"p ({' '.join(names)}) -> p {' '.join(names)}",
                                **{names[j]: dims[j] for j in range(1, len(dims))})
            return v

        a_wq, a_wk, a_wv = part(2 * KT * D), part(2 * KT * KVD), part(2 * KT * KVD)
        a_xT, a_cT, a_q = part(2 * KT * T), part(2 * KT * T), part(2 * KT * T)
        a_k, a_sel = part(2 * T), part(2 * KV * STACK + 64)
        a_wo, a_oT = part(2 * KT * D), part(2 * KT * T)
        a_qs, a_ks = part(NPAIR * T), part(2 * KV * T)
        wq = view(a_wq, 2, KT, D)
        wk = view(a_wk, 2, KT, KVD)
        wv = view(a_wv, 2, KT, KVD)
        wo = view(a_wo, 2, KT, D)
        xT = view(a_xT, 2, KT, T)
        cT = view(a_cT, 2, KT, T)
        qT = view(a_q, 2, KT, T)
        kT = view(a_k, 2, T)
        sel = view(a_sel, 2, KV, STACK)
        oT = view(a_oT, 2, KT, T)
        qs = view(a_qs, 2, NPAIR, SEQ)
        ks = view(a_ks, 2, KV, 2, SEQ)

        up = view(0, 2, KT, INT)
        fc1 = view(8192, 2, KT, LAT)
        ef = view(10240, 2, LT, D)
        gw = view(12288, 2, KT, NE)
        x2T = view(12352, 2, KT, T)
        hT = view(a_wo, 2, MT, T)
        latT = view(a_oT, 2, LT, T)
        down = view(a_qs, 2, MT, D)

        xall = sb("xall", [P, NSEQ, D])
        ctxb = sb("ctxb", [P, 2, D])
        xn = sb("xn", [P, 2, D])
        probs = sb("probs", [P, 2, 4, 2, T])
        vpad = sb("vpad", [P, 2, KV, 3 * HD])
        onepad = sb("onepad", [P, 3 * HD])
        rden = sb("rden", [P, T])
        onorm = sb("onorm", [P, T])
        raw = sb("raw", [P, 5120])
        raw2 = sb("raw2", [P, 1568])
        expT = sb("expT", [P, LT, LAT])
        over = probs[:, :, :, :, :].rearrange("p u j e t -> p (u j e t)").rearrange("p (n b d) -> p n b d", n=4, b=2)
        relu, hfull, ysum = over[:, 0], over[:, 1], over[:, 2]
        scaled = over[:, 3]
        xg = sb("xg", [P, 2, D])
        gammab = sb("gammab", [P, D])
        betab = sb("betab", [P, D])
        top8 = sb("top8", [P, 2, 8])
        rw = sb("rw", [P, 2])
        mv2 = sb("mv2", [P, 2, 2])
        credit = sb("credit", [P, 18])
        st2 = sb("st2", [P, 2, 6])
        vare2 = sb("vare2", [P, 2])
        rstd2 = sb("rstd2", [P, 2])
        nbias2 = sb("nbias2", [P, 2])
        mx = sb("mx", [P, 2, NPAIR, 2])
        negmax = sb("negmax", [P, 2, MAXROWS, NPAIR])
        maxT = sb("maxT", [MAXROWS * NPAIR, 2, P], FP32R)
        ident = sb("ident", [P, P])
        parity = sb("parity", [P, 2])
        maxsel = sb("maxsel", [P, 2])
        stats = sb("stats", [P, NSEQ, 6])
        mv = sb("mv", [P, NSEQ, 2])
        vare = sb("vare", [P, NSEQ])
        rstd = sb("rstd", [P, NSEQ])
        nbias = sb("nbias", [P, NSEQ])
        mhalf = sb("mhalf", [P, NSEQ])
        gates = sb("gates", [P, 2])
        tgates = sb("tgates", [P, 2])

        def bank(name):
            return stack.enter_context(nc.psum_tensor(name, [P, 512], FP32))

        s_bank = [bank("s_bank0"), bank("s_bank1")]
        st_bank = [bank("st_bank0"), bank("st_bank1")]
        o_bank = [bank("o_bank0"), bank("o_bank1")]
        g_bank = [bank("g_bank0"), bank("g_bank1")]

        x0_in, xrest_in, gates_in = sem("x0_in"), sem("xrest_in"), sem("gates_in")
        ctx_in = sem("ctx_in")
        wq_in, wkv_in, wo_in = sem("wq_in"), sem("wkv_in"), sem("wo_in")
        q_stacked = [sem("q_stacked0"), sem("q_stacked1")]
        max_stacked = [sem("max_stacked0"), sem("max_stacked1")]
        stored = sem("stored")
        ident_zero, ident_ready, pool_const = sem("ident_zero"), sem("ident_ready"), sem("pool_const")
        consts = sem("consts")
        wq_hi, wkv_hi, wo_hi = sem("wq_hi"), sem("wkv_hi"), sem("wo_hi")
        wq_lo, wkv_lo, wo_lo = sem("wq_lo"), sem("wkv_lo"), sem("wo_lo")
        var_ready, rstd_ready = sem("var_ready"), sem("rstd_ready")
        xn_ready = sem("xn_ready")
        tanh_ready = sem("tanh_ready")
        g_full = [sem("g_full0"), sem("g_full1")]
        g_done = [sem("g_done0"), sem("g_done1")]
        g_hi = sem("g_hi")
        s_full, s_free = sem("s_full"), sem("s_free")
        st_full, st_free = sem("st_full"), sem("st_free")
        weighed, o_free = sem("weighed"), sem("o_free")
        rden_ready, oT_hi, oT_lo = sem("rden_ready"), sem("oT_hi"), sem("oT_lo")
        max_split = sem("max_split")
        up_in, small_in, down_in, affine_in = sem("up_in"), sem("small_in"), sem("down_in"), sem("affine_in")
        up_hi, up_lo, down_hi, down_lo = sem("up_hi"), sem("up_lo"), sem("down_hi"), sem("down_lo")
        small_lo = sem("small_lo")
        affine_ready = sem("affine_ready")
        x2n_ready, x2_full, x2_hi, x2_lo = sem("x2n_ready"), sem("x2_full"), sem("x2_hi"), sem("x2_lo")
        up_full, up_free, h_full, h_hi, h_lo = sem("up_full"), sem("up_free"), sem("h_full"), sem("h_hi"), sem("h_lo")
        lat_full, lat_hi, lat_lo, logits_full, rw_ready = (
            sem("lat_full"), sem("lat_hi"), sem("lat_lo"), sem("logits_full"), sem("rw_ready"))
        down_full, y_ready, routed_full, routed_scaled = (
            sem("down_full"), sem("y_ready"), sem("routed_full"), sem("routed_scaled"))
        var2_ready, rstd2_ready, xg_ready, out_ready = (
            sem("var2_ready"), sem("rstd2_ready"), sem("xg_ready"), sem("out_ready"))
        own2 = sem("own2")
        waited = sem("waited")
        own = sem("own")

        def raw_view(t, at, n):
            return t[:, at:at + KT * n].rearrange("p (k n) -> p k n", k=KT)

        def wait_apart(eng, signal, value):
            eng.wait_ge(signal, value)
            eng.sem_inc(waited, 1)

        block = stack.enter_context(nc.Block())

        @block.sync
        def _(sp):
            x_v = x.rearrange("s t d -> t s d")
            sp.dma_start(xall[:, 0:2, :], x_v[:, 0:2, :]).then_inc(x0_in, 16)
            sp.dma_start(raw[:, 0:2048].rearrange("p (k n) -> p k n", k=KT),
                         Wq.rearrange("(k p) n -> p k n", p=P)).then_inc(wq_in, 16)
            sp.dma_start(ctxb[:, :, :], ctx[0:2].rearrange("s t d -> t s d")).then_inc(ctx_in, 16)
            sp.dma_start(raw[:, 2048:2560].rearrange("p (k n) -> p k n", k=KT),
                         Wk.rearrange("(k p) n -> p k n", p=P)).then_inc(wkv_in, 16)
            sp.dma_start(raw[:, 2560:3072].rearrange("p (k n) -> p k n", k=KT),
                         Wv.rearrange("(k p) n -> p k n", p=P)).then_inc(wkv_in, 16)
            sp.dma_start(xall[:, 2:NSEQ, :], x_v[:, 2:NSEQ, :]).then_inc(xrest_in, 16)
            wo_v = Wo.rearrange("(hh j pp r) n -> hh pp j r n", hh=2, j=4, pp=2)
            for hh in range(2):
                for pp in range(2):
                    kt = 2 * hh + pp
                    sp.dma_start(raw[:, 3072 + kt * D:3072 + (kt + 1) * D], wo_v[hh, pp]).then_inc(wo_in, 16)
            sp.dma_start(gates[:, 0:1], g_attn.rearrange("(a b) -> a b", a=1).to_broadcast([P, 1])).then_inc(gates_in, 16)
            sp.dma_start(gates[:, 1:2], g_ffn.rearrange("(a b) -> a b", a=1).to_broadcast([P, 1])).then_inc(gates_in, 16)

            def load_ctx(i, F):
                f = F("cT1")
                wait_apart(sp, g_full[f.bank], f.full())
                sp.dma_start(ctxb[:, :, :], ctx[bass.ds(2 * i, 2)].rearrange("s t d -> t s d")).then_inc(ctx_in, 16)

            def stack_q(b, F, st_done):
                for name in ("q0", "q1"):
                    f = F(name)
                    wait_apart(sp, g_done[f.bank], f.full())
                if st_done is not None:
                    wait_apart(sp, st_full, st_done)
                for term, src in enumerate((0, 0, 1)):
                    for strip in range(4):
                        sp.dma_start(
                            qs[32 * term:32 * term + 32, b, strip:NPAIR:4, :].bitcast(FP32),
                            qT[32 * strip:32 * strip + 32, src, :, b * SEQ:(b + 1) * SEQ].bitcast(FP32),
                        ).then_inc(q_stacked[b], 16)

            def stack_max(b, F):
                f = F(f"mT{b}")
                wait_apart(sp, g_done[f.bank], f.full())
                for r in range(MAXROWS):
                    sp.dma_start(qs[STACK + r:STACK + r + 1, b, :, :].bitcast(FP32),
                                 maxT[r * NPAIR:(r + 1) * NPAIR, b, :].bitcast(FP32)).then_inc(max_stacked[b], 16)

            load_ctx(1, fill_first)
            stack_q(0, fill_first, None)
            stack_q(1, fill_first, None)
            stack_max(0, fill_first)

            sp.wait_ge(wq_lo, 1)
            sp.wait_ge(wkv_lo, 2)
            sp.wait_ge(wo_lo, 1)
            sp.dma_start(raw[:, 0:KT * INT].rearrange("p (k n) -> p k n", k=KT),
                         up_w.rearrange("(k p) n -> p k n", p=P)).then_inc(up_in, 16)
            sp.dma_start(raw[:, KT * INT:KT * (INT + LAT)].rearrange("p (k n) -> p k n", k=KT),
                         fc1_w.rearrange("(k p) n -> p k n", p=P)).then_inc(up_in, 16)
            sp.dma_start(raw2[:, 0:512].rearrange("p (k n) -> p k n", k=LT),
                         expert_w.rearrange("(k p) n -> p k n", p=P)).then_inc(small_in, 16)
            sp.dma_start(raw2[:, 512:1536].rearrange("p (k n) -> p k n", k=LT),
                         fc2_w.rearrange("(k p) n -> p k n", p=P)).then_inc(small_in, 16)
            sp.dma_start(raw2[:, 1536:1568].rearrange("p (k n) -> p k n", k=KT),
                         gate_w.rearrange("(k p) n -> p k n", p=P)).then_inc(small_in, 16)
            sp.dma_start(gammab[:, :], gamma.rearrange("(a b) -> a b", a=1).to_broadcast([P, D])).then_inc(affine_in, 16)
            sp.dma_start(betab[:, :], beta.rearrange("(a b) -> a b", a=1).to_broadcast([P, D])).then_inc(affine_in, 16)

            def body(i, more):
                def F(name):
                    return fill_body(name, i)
                stack_max(1, F)
                stack_q(0, F, 16 * i + 8)
                if more: load_ctx(i + 2, F)
                stack_q(1, F, 16 * i + 16)
                stack_max(0, F)

            with sp.Fori(0, PAIRS - 2) as i:
                body(i, True)
            body(PAIRS - 2, False)
            stack_max(1, fill_last)
            sp.wait_ge(up_hi, 5)
            sp.wait_ge(up_lo, 5)
            sp.dma_start(raw[:, 0:MT * D].rearrange("p (k n) -> p k n", k=MT),
                         down_w.rearrange("(k p) n -> p k n", p=P)).then_inc(down_in, 16)
            with sp.Fori(0, PAIRS) as i:
                wait_apart(sp, out_ready, 2 * i + 2 + 2)
                sp.dma_start(out[bass.ds(2 * i, 2)].rearrange("s t d -> t s d"),
                             xall[:, bass.ds(2 * i, 2), :]).then_inc(stored, 16)
            sp.wait_ge(stored, 16 * PAIRS)

        @block.gpsimd
        def _(pool):
            nc.gpsimd.memset(ident[:, :], 0.0).then_inc(ident_zero, 1)
            pool.wait_ge(ident_zero, 1)
            nc.gpsimd.affine_select(out=ident[:, :], in_=ident[:, :], compare_op=ALU.not_equal, fill=1.0,
                                    base=0, pattern=[[-1, P]], channel_multiplier=1).then_inc(ident_ready, 1)
            nc.gpsimd.memset(mhalf[:, :], -0.5).then_inc(pool_const, 1)
            nc.gpsimd.memset(onepad[:, :], 0.0).then_inc(pool_const, 1)
            pool.wait_ge(pool_const, 2)
            nc.gpsimd.memset(onepad[:, HD:2 * HD], 1.0).then_inc(pool_const, 1)
            nc.gpsimd.memset(vpad[:, :, :, :], 0.0).then_inc(pool_const, 1)
            pool.wait_ge(var_ready, 1)
            nc.gpsimd.tensor_tensor(rstd[:, 0:2], vare[:, 0:2], mhalf[:, 0:2], ALU.pow).then_inc(rstd_ready, 1)
            pool.wait_ge(var_ready, 2)
            nc.gpsimd.tensor_tensor(rstd[:, 2:NSEQ], vare[:, 2:NSEQ], mhalf[:, 2:NSEQ], ALU.pow).then_inc(rstd_ready, 1)
            pool.wait_ge(wo_in, 64)
            pool.wait_ge(wo_hi, 1)
            nc.gpsimd.tensor_tensor(wo[:, 1], raw_view(raw, 3072, D), wo[:, 0].bitcast(FP32),
                                    ALU.subtract).then_inc(wo_lo, 1)
            pool.wait_ge(affine_in, 32)
            pool.wait_ge(tanh_ready, 1)
            for t in (gammab, betab):
                nc.gpsimd.tensor_scalar(t[:, :], t[:, :], tgates[:, 1:2], None, ALU.mult).then_inc(affine_ready, 1)
            def inverse_std(value):
                pool.wait_ge(var2_ready, value)
                nc.gpsimd.tensor_tensor(rstd2[:, :], vare2[:, :], mhalf[:, 0:2], ALU.pow).then_inc(rstd2_ready, 1)

            def body(i, more):
                pool.wait_ge(affine_ready, 2)
                for b in range(2):
                    pool.wait_ge(out_ready, 2 * i + b + 1)
                    nc.gpsimd.tensor_tensor(xg[:, b:b + 1, :], xall[:, bass.ds(2 * i + b, 1), :],
                                            betab[:, :].unsqueeze(1), ALU.add).then_inc(xg_ready, 1)
                if more:
                    inverse_std(2 * i + 2)
                inverse_std(2 * i + (3 if more else 2))

            inverse_std(1)
            for k in range(MT // 2, MT):
                pool.wait_ge(down_hi, k + 1)
                nc.gpsimd.tensor_tensor(down[:, 1, k, :], raw[:, k * D:(k + 1) * D], down[:, 0, k, :].bitcast(FP32),
                                        ALU.subtract).then_inc(down_lo, 1)

            f = fill_last("o1")
            pool.wait_ge(g_done[f.bank], f.full())
            with pool.Fori(0, PAIRS - 1) as i:
                body(i, True)
            body(PAIRS - 1, False)

        @block.scalar
        def _(act):
            act.wait_ge(wq_in, 16)
            nc.scalar.activation(wq[:, 0], raw_view(raw, 0, D), ACT.Copy).then_inc(wq_hi, 1)
            act.wait_ge(wkv_in, 32)
            nc.scalar.activation(wk[:, 0], raw_view(raw, 2048, KVD), ACT.Copy).then_inc(wkv_hi, 1)
            nc.scalar.activation(wv[:, 0], raw_view(raw, 2560, KVD), ACT.Copy).then_inc(wkv_hi, 1)

            def take_hi(name, F, dst, src_cols=512):
                f = F(name)
                act.wait_ge(g_full[f.bank], f.full())
                nc.scalar.activation(dst, g_bank[f.bank][:, 0:src_cols] if len(dst.shape) == 2 else
                                     g_bank[f.bank][:, 0:src_cols].rearrange("p (k t) -> p k t", k=dst.shape[1]),
                                     ACT.Copy).then_inc(g_hi, 1)

            def hi_of(name, F):
                if name[:2] in ("xT", "cT"):
                    b = int(name[2])
                    take_hi(name, F, (xT if name[0] == "x" else cT)[:, 0, :, b * SEQ:(b + 1) * SEQ])
                elif name[0] == "q":
                    m = 2 * int(name[1])
                    take_hi(name, F, qT[:, 0, m:m + 2, :])
                elif name == "k":
                    take_hi(name, F, kT[:, 0, :], T)

            def spread_k(n, F):
                f = F(f"K{n}")
                act.wait_ge(g_full[f.bank], f.full())
                for par in range(2):
                    last = nc.scalar.activation(
                        ks[0:STACK, :, 2 * n:2 * n + 2, par, :],
                        g_bank[f.bank][0:STACK, :].rearrange("p (h s t) -> p s h t", h=2, s=2),
                        ACT.Copy, scale=parity[0:STACK, par:par + 1])
                last.then_inc(g_done[f.bank], 1)

            def take_v(F):
                f = F("V")
                act.wait_ge(g_full[f.bank], f.full())
                nc.scalar.activation(vpad[:, :, :, HD:2 * HD],
                                     g_bank[f.bank][:, 0:T].rearrange("p (s h d) -> p s h d", s=2, h=KV),
                                     ACT.Copy).then_inc(g_done[f.bank], 1)

            def take_max(b, F):
                f = F(f"mT{b}")
                act.wait_ge(g_full[f.bank], f.full())
                nc.scalar.activation(maxT[:, b, :], g_bank[f.bank][0:MAXROWS * NPAIR, 0:P],
                                     ACT.Copy).then_inc(g_done[f.bank], 1)

            def exp_step(i, t):
                act.wait_ge(st_full, 16 * i + t + 1)
                g = t // 4
                if t % 4 == 0:
                    act.wait_ge(weighed, 4 * i + g + 1)
                nc.scalar.activation(probs[:, g % 2, t % 4, :, :],
                                     st_bank[t % 2][:, :].rearrange("p (a b) -> p a b", a=2),
                                     ACT.Exp, scale=SCALE).then_inc(st_free, 1)

            for name in SPLIT:
                hi_of(name, fill_first)
            act.wait_ge(consts, 1)
            spread_k(0, fill_first)
            spread_k(2, fill_first)
            act.wait_ge(pool_const, 4)
            take_v(fill_first)
            act.wait_ge(wo_in, 64)
            nc.scalar.activation(wo[:, 0], raw_view(raw, 3072, D), ACT.Copy).then_inc(wo_hi, 1)
            act.wait_ge(gates_in, 32)
            nc.scalar.activation(tgates[:, :], gates[:, :], ACT.Tanh).then_inc(tanh_ready, 1)
            take_max(0, fill_first)
            with act.Fori(0, PAIRS - 1) as i:
                def F(name):
                    return fill_body(name, i)
                for t in range(16):
                    exp_step(i, t)
                    if t == 1: hi_of("xT0", F)
                    if t == 2: hi_of("xT1", F)
                    if t == 3: take_max(1, F)
                    if t == 5: hi_of("cT0", F)
                    if t == 6: hi_of("cT1", F)
                    if t == 7:
                        for b in range(2):
                            act.wait_ge(q_stacked[b], 192 * (i + 1))
                        hi_of("q0", F)
                    if t == 9: hi_of("q1", F)
                    if t == 11: hi_of("k", F)
                spread_k(0, F)
                spread_k(2, F)
                take_v(F)
                take_max(0, F)
            for t in range(16):
                exp_step(PAIRS - 1, t)
                if t == 3: take_max(1, fill_last)
                if t == 4:
                    for name in ("V", "K3"):
                        f = fill_body(name, PAIRS - 2)
                        act.wait_ge(g_full[f.bank], f.full())
                    for b in range(2):
                        act.wait_ge(q_stacked[b], 192 * PAIRS)
                    act.wait_ge(up_in, 32)
                    act.wait_ge(small_in, 48)
                if 4 <= t < 8:
                    k = t - 4
                    nc.scalar.activation(up[:, 0, k, :], raw[:, k * INT:(k + 1) * INT], ACT.Copy).then_inc(up_hi, 1)
                if t == 8:
                    nc.scalar.activation(fc1[:, 0], raw_view(raw, KT * INT, LAT), ACT.Copy)
                    nc.scalar.activation(gw[:, 0], raw_view(raw2, 1536, NE), ACT.Copy).then_inc(up_hi, 1)
                if t == 9:
                    f = fill_last("eT")
                    act.wait_ge(g_full[f.bank], f.full())
                    nc.scalar.activation(expT[:, :, :], g_bank[f.bank][:, :].rearrange("p (k n) -> p k n", k=LT),
                                         ACT.Copy).then_inc(g_done[f.bank], 1)
                if t in (11, 12):
                    f = fill_last(f"ef{t - 11}")
                    act.wait_ge(g_full[f.bank], f.full())
                    nc.scalar.activation(ef[:, 0, t - 11, :], g_bank[f.bank][:, :], ACT.Copy).then_inc(g_hi, 1)

            def x2_hi_part(i, b):
                act.wait_ge(x2_full, 2 * i + b + 1)
                nc.scalar.activation(x2T[:, 0, :, b * SEQ:(b + 1) * SEQ],
                                     st_bank[b][:, :].rearrange("p (k t) -> p k t", k=KT), ACT.Copy).then_inc(x2_hi, 1)

            for b in range(2):
                x2_hi_part(0, b)
            act.wait_ge(down_in, 16)
            act.wait_ge(st_full, 16 * PAIRS)
            for k in range(MT):
                nc.scalar.activation(down[:, 0, k, :], raw[:, k * D:(k + 1) * D], ACT.Copy).then_inc(down_hi, 1)

            def ffn(i, more):
                for u in range(MT // 2):
                    act.wait_ge(up_full, 4 * i + u + 1)
                    nc.scalar.activation(relu[:, u % 2, :], s_bank[u % 2][:, :], ACT.Relu).then_inc(up_free, 1)
                    act.wait_ge(up_free, 4 * i + u + 1 + 2)
                    act.wait_ge(h_lo, 4 * i + u + 1)
                    nc.scalar.activation(hfull[:, u % 2, :], relu[:, u % 2, :], ACT.Square).then_inc(h_full, 1)
                act.wait_ge(lat_full, i + 1)
                nc.scalar.activation(latT[:, 0], o_bank[0][:, :].rearrange("p (k t) -> p k t", k=LT),
                                     ACT.Copy).then_inc(lat_hi, 1)
                if more:
                    for b in range(2):
                        x2_hi_part(i + 1, b)
                for b in range(2):
                    act.wait_ge(routed_full, 2 * i + b + 1)
                    act.wait_ge(rw_ready, i + 1)
                    act.wait_ge(y_ready, 2 * i + b + 1)
                    nc.scalar.activation(scaled[:, b, :], o_bank[b][:, :], ACT.Copy,
                                         scale=rw[:, b:b + 1]).then_inc(routed_scaled, 1)

            with act.Fori(0, PAIRS - 1) as i:
                ffn(i, True)
            ffn(PAIRS - 1, False)

        @block.vector
        def _(dve):
            count = [0]

            def mine(ins):
                count[0] += 1
                ins.then_inc(own, 1)
                dve.wait_ge(own, count[0])

            nc.vector.memset(store[:, a_sel:a_sel + 2 * KV * STACK].bitcast(FP32), 0.0).then_inc(own, 1)
            count[0] += 1
            for n, free in enumerate((s_free, st_free, o_free, weighed, up_free, h_lo, y_ready, routed_scaled, out_ready)):
                for m in range(2):
                    nc.vector.memset(credit[:, 2 * n + m:2 * n + m + 1], 0.0).then_inc(free, 1)

            def ln_stats(lo, hi, which):
                for s in range(lo, hi):
                    last = nc.vector.bn_stats(stats[:, s, :], xall[:, s, :])
                mine(last)
                for s in range(lo, hi):
                    last = nc.vector.bn_aggr(mv[:, s, :], stats[:, s, :])
                mine(last)
                nc.vector.tensor_scalar(vare[:, lo:hi], mv[:, lo:hi, 1], EPS, None, ALU.add).then_inc(var_ready, 1)
                dve.wait_ge(rstd_ready, which)
                mine(nc.vector.scalar_tensor_tensor(out=nbias[:, lo:hi], in0=mv[:, lo:hi, 0], scalar=-1.0,
                                                    in1=rstd[:, lo:hi], op0=ALU.mult, op1=ALU.mult))

            def normalize(i):
                for b in range(2):
                    nc.vector.tensor_scalar(xn[:, b:b + 1, :], xall[:, bass.ds(2 * i + b, 1), :],
                                            rstd_col(rstd, i, b), rstd_col(nbias, i, b),
                                            ALU.mult, ALU.add).then_inc(xn_ready, 1)

            def rstd_col(t, i, b):
                return t[:, bass.ds(2 * i + b, 1)]

            def take_lo(name, F, a):
                f = F(name)
                dve.wait_ge(g_hi, len(SPLIT) * a + SPLIT.index(name) + 1)
                if name[:2] in ("xT", "cT"):
                    b = int(name[2])
                    t = xT if name[0] == "x" else cT
                    dst, hi = t[:, 1, :, b * SEQ:(b + 1) * SEQ], t[:, 0, :, b * SEQ:(b + 1) * SEQ]
                    src = g_bank[f.bank][:, :].rearrange("p (k t) -> p k t", k=KT)
                elif name[0] == "q":
                    m = 2 * int(name[1])
                    dst, hi = qT[:, 1, m:m + 2, :], qT[:, 0, m:m + 2, :]
                    src = g_bank[f.bank][:, :].rearrange("p (k t) -> p k t", k=2)
                else:
                    dst, hi, src = kT[:, 1, :], kT[:, 0, :], g_bank[f.bank][:, 0:T]
                nc.vector.tensor_tensor(dst, src, hi.bitcast(FP32), ALU.subtract).then_inc(g_done[f.bank], 1)

            def spread_k(n, F):
                f = F(f"K{n}")
                dve.wait_ge(g_full[f.bank], f.full())
                for par in range(2):
                    last = nc.vector.tensor_scalar(
                        ks[0:STACK, :, 2 * n:2 * n + 2, par, :],
                        g_bank[f.bank][0:STACK, :].rearrange("p (h s t) -> p s h t", h=2, s=2),
                        parity[0:STACK, par:par + 1], None, ALU.mult)
                last.then_inc(g_done[f.bank], 1)

            def row_max(i, s):
                dve.wait_ge(s_full, 16 * i + s + 1)
                b, h = s // 8, s % 8
                nc.vector.reduce_max(mx[:, b, 2 * h:2 * h + 2, :],
                                     s_bank[s % 2][:, :].rearrange("p (a e k) -> p a e k", a=2, e=2),
                                     AX.X).then_inc(s_free, 1)

            def split_max(i, b):
                dve.wait_ge(s_free, 16 * i + 8 * b + 8 + 2)
                v = negmax[:, b].rearrange("p (e l) n -> p e l n", e=2)
                m = mx[:, b].rearrange("p n e -> p e n")
                nc.vector.tensor_scalar(v[:, :, 0, :].bitcast(FP32R), m, -1.0, None, ALU.mult).then_inc(max_split, 1)
                dve.wait_ge(max_split, 4 * i + 2 * b + 1)
                nc.vector.scalar_tensor_tensor(out=v[:, :, 1, :].bitcast(FP32R), in0=m, scalar=-1.0,
                                               in1=v[:, :, 0, :], op0=ALU.mult, op1=ALU.subtract).then_inc(max_split, 1)

            def head_outputs(i, g):
                b, hh = g // 2, g % 2
                bank = o_bank[g % 2]
                dve.wait_ge(weighed, 4 * i + g + 1 + 2)
                nc.vector.reciprocal(rden[:, :], bank[:, T:2 * T]).then_inc(rden_ready, 1)
                dve.wait_ge(rden_ready, 4 * i + g + 1)
                nc.vector.tensor_tensor(onorm[:, :], bank[:, 0:T], rden[:, :], ALU.mult).then_inc(o_free, 1)
                dve.wait_ge(o_free, 4 * i + g + 1 + 2)
                on = onorm[:, :].rearrange("p (k t) -> p k t", k=2)
                hi = oT[:, 0, 2 * hh:2 * hh + 2, b * SEQ:(b + 1) * SEQ]
                nc.vector.tensor_copy(hi, on).then_inc(oT_hi, 1)
                dve.wait_ge(oT_hi, 4 * i + g + 1)
                nc.vector.tensor_tensor(oT[:, 1, 2 * hh:2 * hh + 2, b * SEQ:(b + 1) * SEQ], on,
                                        hi.bitcast(FP32), ALU.subtract).then_inc(oT_lo, 1)

            def add_attention(i, b, F):
                f = F(f"o{b}")
                dve.wait_ge(g_full[f.bank], f.full())
                xb = xall[:, bass.ds(2 * i + b, 1), :].rearrange("p a d -> p (a d)")
                nc.vector.scalar_tensor_tensor(out=xb, in0=g_bank[f.bank][:, :], scalar=tgates[:, 0:1], in1=xb,
                                               op0=ALU.mult, op1=ALU.add).then_inc(g_done[f.bank], 1)

            dve.wait_ge(x0_in, 16)
            ln_stats(0, 2, 1)
            normalize(0)
            dve.wait_ge(wq_hi, 1)
            nc.vector.tensor_tensor(wq[:, 1], raw_view(raw, 0, D), wq[:, 0].bitcast(FP32), ALU.subtract).then_inc(wq_lo, 1)
            dve.wait_ge(ident_ready, 1)
            id_v = ident[:, :].rearrange("p (h d) -> p h d", h=KV)
            for term, part_ in enumerate((0, 1, 0)):
                for par in range(2):
                    last = nc.vector.tensor_copy(
                        sel[:, part_, :, (2 * term + par) * HD:(2 * term + par + 1) * HD], id_v)
            last.then_inc(consts, 1)
            for par in range(2):
                nc.vector.reduce_sum(parity[:, par:par + 1],
                                     ident[:, :].rearrange("p (a e d) -> p e a d", e=2, d=HD)[:, par],
                                     AX.XY)
                last = nc.vector.reduce_sum(maxsel[:, par:par + 1],
                                            ident[:, STACK + 2 * par:STACK + 2 * par + 2], AX.X)
            mine(last)
            for par in range(2):
                last = nc.vector.tensor_scalar(
                    ks[STACK:P, :, :, par, :].rearrange("p s h t -> p (s h) t"),
                    ident[STACK:P, 0:1].unsqueeze(2).to_broadcast([32, 2 * KV, SEQ]), 0.0,
                    maxsel[STACK:P, par:par + 1], ALU.mult, ALU.add)
            last.then_inc(consts, 1)
            dve.wait_ge(wkv_hi, 2)
            nc.vector.tensor_tensor(wk[:, 1], raw_view(raw, 2048, KVD), wk[:, 0].bitcast(FP32), ALU.subtract).then_inc(wkv_lo, 1)
            nc.vector.tensor_tensor(wv[:, 1], raw_view(raw, 2560, KVD), wv[:, 0].bitcast(FP32), ALU.subtract).then_inc(wkv_lo, 1)
            for name in SPLIT:
                take_lo(name, fill_first, 0)
            spread_k(1, fill_first)
            spread_k(3, fill_first)
            dve.wait_ge(xrest_in, 16)
            ln_stats(2, NSEQ, 2)
            for s in range(16):
                row_max(0, s)
                if s == 7: split_max(0, 0)
            split_max(0, 1)
            dve.wait_ge(tanh_ready, 1)
            with dve.Fori(0, PAIRS - 1) as i:
                def F(name):
                    return fill_body(name, i)
                normalize(i + 1)
                take_lo("xT0", F, i + 1)
                take_lo("xT1", F, i + 1)
                head_outputs(i, 0)
                take_lo("cT0", F, i + 1)
                take_lo("cT1", F, i + 1)
                take_lo("q0", F, i + 1)
                head_outputs(i, 1)
                take_lo("q1", F, i + 1)
                take_lo("k", F, i + 1)
                head_outputs(i, 2)
                spread_k(1, F)
                head_outputs(i, 3)
                spread_k(3, F)
                for s in range(16):
                    row_max(i + 1, s)
                    if s == 3: add_attention(i, 0, F)
                    if s == 7: split_max(i + 1, 0)
                    if s == 11: add_attention(i, 1, F)
                split_max(i + 1, 1)

            seen = [0]

            def chained(ins, i):
                seen[0] += 1
                ins.then_inc(own2, 1)
                wait_apart(dve, own2, OWN2 * i + seen[0])

            def inverse_std(src, i, which):
                for b in range(2):
                    last = nc.vector.bn_stats(st2[:, b, :], src(b))
                chained(last, i)
                for b in range(2):
                    last = nc.vector.bn_aggr(mv2[:, b, :], st2[:, b, :])
                chained(last, i)
                nc.vector.tensor_scalar(vare2[:, :], mv2[:, :, 1], EPS, None, ALU.add).then_inc(var2_ready, 1)
                dve.wait_ge(rstd2_ready, which)

            def normalize2(i, which, a):
                inverse_std(lambda b: xall[:, bass.ds(2 * a + b, 1), :].rearrange("p a d -> p (a d)"), i, which)
                chained(nc.vector.scalar_tensor_tensor(out=nbias2[:, :], in0=mv2[:, :, 0], scalar=-1.0,
                                                       in1=rstd2[:, :], op0=ALU.mult, op1=ALU.mult), i)
                for b in range(2):
                    nc.vector.tensor_scalar(xn[:, b:b + 1, :], xall[:, bass.ds(2 * a + b, 1), :],
                                            rstd2[:, b:b + 1], nbias2[:, b:b + 1],
                                            ALU.mult, ALU.add).then_inc(x2n_ready, 1)

            def x2_lo_part(i, b):
                dve.wait_ge(x2_hi, 2 * i + b + 1)
                nc.vector.tensor_tensor(x2T[:, 1, :, b * SEQ:(b + 1) * SEQ],
                                        st_bank[b][:, :].rearrange("p (k t) -> p k t", k=KT),
                                        x2T[:, 0, :, b * SEQ:(b + 1) * SEQ].bitcast(FP32),
                                        ALU.subtract).then_inc(x2_lo, 1)

            normalize2(0, 1, 0)
            head_outputs(PAIRS - 1, 0)
            for k in range(KT):
                dve.wait_ge(up_hi, k + 1)
                nc.vector.tensor_tensor(up[:, 1, k, :], raw[:, k * INT:(k + 1) * INT],
                                        up[:, 0, k, :].bitcast(FP32), ALU.subtract).then_inc(up_lo, 1)
                if k == 1: head_outputs(PAIRS - 1, 1)
            dve.wait_ge(up_hi, 5)
            nc.vector.tensor_tensor(fc1[:, 1], raw_view(raw, KT * INT, LAT), fc1[:, 0].bitcast(FP32),
                                    ALU.subtract).then_inc(up_lo, 1)
            nc.vector.tensor_tensor(gw[:, 1], raw_view(raw2, 1536, NE), gw[:, 0].bitcast(FP32),
                                    ALU.subtract).then_inc(small_lo, 1)
            head_outputs(PAIRS - 1, 2)
            for l in range(LT):
                f = fill_last(f"ef{l}")
                dve.wait_ge(g_hi, len(SPLIT) * PAIRS + l + 1)
                nc.vector.tensor_tensor(ef[:, 1, l, :], g_bank[f.bank][:, :], ef[:, 0, l, :].bitcast(FP32),
                                        ALU.subtract).then_inc(g_done[f.bank], 1)
            head_outputs(PAIRS - 1, 3)
            for b in range(2):
                x2_lo_part(0, b)
            for b in range(2):
                add_attention(PAIRS - 1, b, fill_last)
            for k in range(MT // 2):
                dve.wait_ge(down_hi, k + 1)
                nc.vector.tensor_tensor(down[:, 1, k, :], raw[:, k * D:(k + 1) * D], down[:, 0, k, :].bitcast(FP32),
                                        ALU.subtract).then_inc(down_lo, 1)

            start2 = seen[0]

            def ffn(i, more):
                seen[0] = start2
                if more:
                    normalize2(i, 2 * i + 2, i + 1)
                for u in range(MT // 2):
                    dve.wait_ge(h_full, 4 * i + u + 1)
                    src = hfull[:, u % 2, :].rearrange("p (m t) -> p m t", m=2)
                    nc.vector.tensor_copy(hT[:, 0, 2 * u:2 * u + 2, :], src).then_inc(h_hi, 1)
                    dve.wait_ge(h_hi, 4 * i + u + 1)
                    nc.vector.tensor_tensor(hT[:, 1, 2 * u:2 * u + 2, :], src,
                                            hT[:, 0, 2 * u:2 * u + 2, :].bitcast(FP32), ALU.subtract).then_inc(h_lo, 1)
                dve.wait_ge(lat_hi, i + 1)
                nc.vector.tensor_tensor(latT[:, 1], o_bank[0][:, :].rearrange("p (k t) -> p k t", k=LT),
                                        latT[:, 0].bitcast(FP32), ALU.subtract).then_inc(lat_lo, 1)
                wait_apart(dve, logits_full, i + 1)
                for b in range(2):
                    last = nc.vector.max(top8[:, b, :], o_bank[1][:, b * NE:(b + 1) * NE])
                chained(last, i)
                nc.vector.tensor_tensor(rw[:, :], top8[:, :, 0], top8[:, :, 1], ALU.add).then_inc(rw_ready, 1)
                if more:
                    for b in range(2):
                        x2_lo_part(i + 1, b)
                for b in range(2):
                    dve.wait_ge(down_full, 2 * i + b + 1)
                    dve.wait_ge(routed_scaled, 2 * i + b + 1 + 2)
                    nc.vector.tensor_tensor(ysum[:, b, :], g_bank[b][:, :], scaled[:, b, :], ALU.add).then_inc(y_ready, 1)
                dve.wait_ge(y_ready, 2 * i + 2 + 2)
                inverse_std(lambda b: ysum[:, b, :], i, 2 * i + (3 if more else 2))
                dve.wait_ge(affine_ready, 2)
                for b in range(2):
                    last = nc.vector.scalar_tensor_tensor(out=ysum[:, b, :], in0=ysum[:, b, :], scalar=mv2[:, b, 0:1],
                                                          in1=gammab[:, :], op0=ALU.subtract, op1=ALU.mult)
                chained(last, i)
                dve.wait_ge(xg_ready, 2 * i + 2)
                for b in range(2):
                    nc.vector.scalar_tensor_tensor(out=xall[:, bass.ds(2 * i + b, 1), :].rearrange("p a d -> p (a d)"),
                                                   in0=ysum[:, b, :], scalar=rstd2[:, b:b + 1], in1=xg[:, b, :],
                                                   op0=ALU.mult, op1=ALU.add).then_inc(out_ready, 1)

            with dve.Fori(0, PAIRS - 1) as i:
                ffn(i, True)
                assert seen[0] == start2 + OWN2
            ffn(PAIRS - 1, False)

        @block.tensor
        def _(pe):
            def claim(name, F):
                f = F(name)
                if not (isinstance(f.earlier(), int) and f.earlier() == 0):
                    pe.wait_ge(g_done[f.bank], f.earlier())
                return f

            def ready(name, F):
                f = F(name)
                pe.wait_ge(g_done[f.bank], f.full())

            def transposed(name, F, src):
                f = claim(name, F)
                for k in range(KT):
                    last = nc.tensor.transpose(g_bank[f.bank][:, k * P:(k + 1) * P], src[:, k * P:(k + 1) * P],
                                               ident[:, :])
                last.then_inc(g_full[f.bank], 1)

            def three(dst, lhs, rhs, tiles):
                n = 0
                for k in range(tiles):
                    for a, c in ((0, 0), (0, 1), (1, 0)):
                        last = nc.tensor.matmul(dst, lhs(a, k), rhs(c, k), start=(n == 0), stop=(n == 3 * tiles - 1))
                        n += 1
                return last

            def project_q(n, F):
                f = claim(f"q{n}", F)
                for m in range(2):
                    cols = (2 * n + m) * P
                    last = three(g_bank[f.bank][:, m * T:(m + 1) * T], lambda a, k: wq[:, a, k, cols:cols + P],
                                 lambda c, k: xT[:, c, k, :], KT)
                last.then_inc(g_full[f.bank], 1)

            def project_k(F):
                f = claim("k", F)
                three(g_bank[f.bank][:, 0:T], lambda a, k: wk[:, a, k, :], lambda c, k: cT[:, c, k, :],
                      KT).then_inc(g_full[f.bank], 1)

            def project_v(F):
                f = claim("V", F)
                for b in range(2):
                    last = three(g_bank[f.bank][:, b * KVD:(b + 1) * KVD],
                                 lambda a, k: cT[:, a, k, b * SEQ:(b + 1) * SEQ], lambda c, k: wv[:, c, k, :], KT)
                last.then_inc(g_full[f.bank], 1)

            def select_k(n, F):
                f = claim(f"K{n}", F)
                for h in range(2):
                    dst = g_bank[f.bank][0:STACK, h * T:(h + 1) * T]
                    nc.tensor.matmul(dst, sel[:, 0, 2 * n + h, :], kT[:, 0, :], start=True, stop=False)
                    last = nc.tensor.matmul(dst, sel[:, 1, 2 * n + h, :], kT[:, 1, :], start=False, stop=True)
                last.then_inc(g_full[f.bank], 1)

            def scores(i, s):
                b, h = s // 8, s % 8
                pe.wait_ge(s_free, 16 * i + s + 1)
                for p in range(2):
                    last = nc.tensor.matmul(s_bank[s % 2][:, p * T:(p + 1) * T], qs[0:STACK, b, 2 * h + p, :],
                                            ks[0:STACK, b, h, :, :], start=True, stop=True)
                last.then_inc(s_full, 1)

            def transpose_max(i, b, F):
                f = claim(f"mT{b}", F)
                wait_apart(pe, max_split, 4 * i + 2 * b + 2)
                nc.tensor.transpose(g_bank[f.bank][0:MAXROWS * NPAIR, 0:P],
                                    negmax[:, b].rearrange("p r n -> p (r n)"), ident[:, :]).then_inc(g_full[f.bank], 1)

            def scores_t(i, t):
                b, h = t // 8, t % 8
                if h == 0:
                    pe.wait_ge(max_stacked[b], 16 * MAXROWS * (i + 1))
                pe.wait_ge(st_free, 16 * i + t + 1)
                for par in range(2):
                    last = nc.tensor.matmul(st_bank[t % 2][:, par * T:(par + 1) * T],
                                            ks[0:STACK + MAXROWS, b, h, par, :],
                                            qs[0:STACK + MAXROWS, b, 2 * h:2 * h + 2, :], start=True, stop=True)
                last.then_inc(st_full, 1)

            def weigh_values(i, g):
                b, hh = g // 2, g % 2
                bank = o_bank[g % 2]
                pe.wait_ge(st_free, 16 * i + 4 * g + 4 + 2)
                pe.wait_ge(o_free, 4 * i + g + 1)
                for what in range(2):
                    for par in range(2):
                        for j in range(4):
                            lo = HD * (1 - par)
                            w = vpad[:, b, 4 * hh + j, lo:lo + 2 * HD] if what == 0 else onepad[:, lo:lo + 2 * HD]
                            last = nc.tensor.matmul(bank[32 * j:32 * j + 32, what * T:(what + 1) * T], w,
                                                    probs[:, g % 2, j, par, :], start=(par == 0), stop=(par == 1),
                                                    tile_position=(0, 32 * j))
                last.then_inc(weighed, 1)

            def project_out(i, b, F):
                f = claim(f"o{b}", F)
                pe.wait_ge(oT_lo, 4 * i + 2 * b + 2)
                three(g_bank[f.bank][:, :], lambda a, k: oT[:, a, k, b * SEQ:(b + 1) * SEQ],
                      lambda c, k: wo[:, c, k, :], KT).then_inc(g_full[f.bank], 1)

            pe.wait_ge(ident_ready, 1)
            for b in range(2):
                pe.wait_ge(xn_ready, b + 1)
                transposed(f"xT{b}", fill_first, xn[:, b, :])
            pe.wait_ge(ctx_in, 16)
            for b in range(2):
                transposed(f"cT{b}", fill_first, ctxb[:, b, :])
            ready("xT0", fill_first)
            ready("xT1", fill_first)
            pe.wait_ge(wq_lo, 1)
            project_q(0, fill_first)
            project_q(1, fill_first)
            ready("cT0", fill_first)
            ready("cT1", fill_first)
            pe.wait_ge(wkv_lo, 2)
            project_k(fill_first)
            ready("k", fill_first)
            pe.wait_ge(consts, 2)
            for n in range(4):
                select_k(n, fill_first)
            project_v(fill_first)
            for n in range(4):
                ready(f"K{n}", fill_first)
            for s in range(16):
                if s % 8 == 0:
                    pe.wait_ge(q_stacked[s // 8], 192)
                scores(0, s)
                if s == 9: transpose_max(0, 0, fill_first)
            pe.wait_ge(pool_const, 4)
            with pe.Fori(0, PAIRS - 1) as i:
                def F(name):
                    return fill_body(name, i)
                for t in range(16):
                    scores_t(i, t)
                    if t == 2:
                        pe.wait_ge(xn_ready, 2 * i + 3)
                        transposed("xT0", F, xn[:, 0, :])
                    if t == 3:
                        pe.wait_ge(xn_ready, 2 * i + 4)
                        transposed("xT1", F, xn[:, 1, :])
                        transpose_max(i, 1, F)
                    if t == 5:
                        weigh_values(i, 0)
                        pe.wait_ge(ctx_in, 16 * i + 32)
                        transposed("cT0", F, ctxb[:, 0, :])
                    if t == 6: transposed("cT1", F, ctxb[:, 1, :])
                    if t == 7:
                        ready("xT0", F)
                        ready("xT1", F)
                        project_q(0, F)
                    if t == 8: weigh_values(i, 1)
                    if t == 9: project_q(1, F)
                    if t == 11:
                        ready("cT0", F)
                        ready("cT1", F)
                        project_k(F)
                    if t == 12: weigh_values(i, 2)
                ready("k", F)
                select_k(0, F)
                select_k(1, F)
                weigh_values(i, 3)
                select_k(2, F)
                select_k(3, F)
                for n in range(4):
                    ready(f"K{n}", F)
                pe.wait_ge(wo_lo, 1)
                for s in range(16):
                    if s % 8 == 0:
                        pe.wait_ge(q_stacked[s // 8], 192 * i + 384)
                    scores(i + 1, s)
                    if s == 1: project_v(F)
                    if s == 3: project_out(i, 0, F)
                    if s == 9: transpose_max(i + 1, 0, F)
                    if s == 11: project_out(i, 1, F)
            last_pair = PAIRS - 1

            def transpose_x2(i, b):
                pe.wait_ge(x2n_ready, 2 * i + b + 1)
                for k in range(KT):
                    last = nc.tensor.transpose(st_bank[b][:, k * P:(k + 1) * P], xn[:, b, k * P:(k + 1) * P], ident[:, :])
                last.then_inc(x2_full, 1)

            for t in range(16):
                scores_t(last_pair, t)
                if t == 3: transpose_max(last_pair, 1, fill_last)
                if t in WEIGH_AFTER: weigh_values(last_pair, WEIGH_AFTER[t])
                if t == 6:
                    f = claim("eT", fill_last)
                    pe.wait_ge(small_in, 48)
                    for m in range(LT):
                        for l in range(LT):
                            last = nc.tensor.transpose(g_bank[f.bank][:, (2 * m + l) * P:(2 * m + l + 1) * P],
                                                       raw2[:, l * LAT + m * P:l * LAT + (m + 1) * P], ident[:, :])
                    last.then_inc(g_full[f.bank], 1)
                if t == 10:
                    ready("eT", fill_last)
                    for l in range(LT):
                        f = claim(f"ef{l}", fill_last)
                        for m in range(LT):
                            last = nc.tensor.matmul(g_bank[f.bank][:, :], expT[:, m, l * P:(l + 1) * P],
                                                    raw2[:, 512 + m * D:512 + (m + 1) * D],
                                                    start=(m == 0), stop=(m == LT - 1))
                        last.then_inc(g_full[f.bank], 1)
            pe.wait_ge(st_free, 16 * PAIRS + 2)
            for b in range(2):
                transpose_x2(0, b)
            weigh_values(last_pair, 3)
            for b in range(2):
                project_out(last_pair, b, fill_last)

            pe.wait_ge(s_free, 16 * PAIRS + 2)
            pe.wait_ge(o_free, 4 * PAIRS + 2)
            pe.wait_ge(up_lo, 5)
            pe.wait_ge(small_lo, 1)
            ready("ef0", fill_last)
            ready("ef1", fill_last)

            def ffn(i, more):
                pe.wait_ge(x2_lo, 2 * i + 2)
                for u in range(MT // 2):
                    pe.wait_ge(up_free, 4 * i + u + 1)
                    for m in range(2):
                        cols = (2 * u + m) * P
                        last = three(s_bank[u % 2][:, m * T:(m + 1) * T], lambda a, k: up[:, a, k, cols:cols + P],
                                     lambda c, k: x2T[:, c, k, :], KT)
                    last.then_inc(up_full, 1)
                pe.wait_ge(routed_scaled, 2 * i + 2)
                for m in range(LT):
                    last = three(o_bank[0][:, m * T:(m + 1) * T], lambda a, k: fc1[:, a, k, m * P:(m + 1) * P],
                                 lambda c, k: x2T[:, c, k, :], KT)
                last.then_inc(lat_full, 1)
                for b in range(2):
                    last = three(o_bank[1][:, b * NE:(b + 1) * NE], lambda a, k: x2T[:, a, k, b * SEQ:(b + 1) * SEQ],
                                 lambda c, k: gw[:, c, k, :], KT)
                last.then_inc(logits_full, 1)
                if more:
                    for b in range(2):
                        transpose_x2(i + 1, b)
                pe.wait_ge(down_lo, MT)
                pe.wait_ge(h_lo, 4 * i + 4 + 2)
                for b in range(2):
                    pe.wait_ge(y_ready, 2 * i + b + 1)
                    three(g_bank[b][:, :], lambda a, k: hT[:, a, k, b * SEQ:(b + 1) * SEQ],
                          lambda c, k: down[:, c, k, :], MT).then_inc(down_full, 1)
                pe.wait_ge(lat_lo, i + 1)
                pe.wait_ge(rw_ready, i + 1)
                for b in range(2):
                    three(o_bank[b][:, :], lambda a, k: latT[:, a, k, b * SEQ:(b + 1) * SEQ],
                          lambda c, k: ef[:, c, k, :], LT).then_inc(routed_full, 1)

            with pe.Fori(0, PAIRS - 1) as i:
                ffn(i, True)
            ffn(PAIRS - 1, False)


_INS = ['x', 'ctx_4096', 'g_xattn', 'g_ffn', 'L0_xattn_Wq', 'L0_xattn_Wk', 'L0_xattn_Wv', 'L0_xattn_Wo',
        'L0_ffn_gate_w', 'L0_ffn_up_w', 'L0_ffn_down_w', 'L0_ffn_fc1_w', 'L0_ffn_fc2_w', 'L0_ffn_expert_w',
        'L0_ffn_ln_gamma', 'L0_ffn_ln_beta']
_OUT = ((8, 128, 512), 'float32')


def kernel(**inputs):
    import numpy as _np
    import concourse.bacc as _bacc
    from concourse.bass_utils import run_bass_kernel_spmd as _run

    nc = _bacc.Bacc("TRN2", target_bir_lowering=False, num_devices=1)
    arrays, args = {}, []
    for name in _INS:
        a = _np.ascontiguousarray(inputs[name])
        arrays[f"in_{name}_dram"] = a
        args.append(nc.dram_tensor(f"in_{name}_dram", a.shape, mybir.dt.from_np(a.dtype), kind="ExternalInput").ap())
    args.append(nc.dram_tensor("out_0_dram", _OUT[0], mybir.dt.from_np(_np.dtype(_OUT[1])), kind="ExternalOutput").ap())
    flamingo_block(nc, *args)
    r = _run(nc, [arrays], core_ids=[0])
    return r.results[0]["out_0_dram"]
```

```python
from contextlib import ExitStack

import concourse.bass as bass
from concourse import mybir

FP32 = mybir.dt.float32
FP32R = mybir.dt.float32r
ALU = mybir.AluOpType
ACT = mybir.ActivationFunctionType
AX = mybir.AxisListType

P = 128
NSEQ = 8
SEQ = 128
D = 512
KT = D // P
HEADS, KV, HD = 32, 8, 16
GROUP = HEADS // KV
NPAIR = HEADS // 2
PAIRS = NSEQ // 2
T = 2 * SEQ
KVD = KV * HD
INT, LAT, NE = 1024, 256, 8
MT = INT // P
LT = LAT // P
STACK = 3 * 2 * HD
MAXROWS = 4
DOWN_EARLY = 5
OWN2 = 9
SCALE = float(HD) ** -0.5
EPS = 1e-5


WARM_START, WARM_STACK, WARM_MAX = 14, 18, 9


class Fill:

    def __init__(self, number, loop=0):
        self.bank, self.before, self.loop = number % 2, number // 2, loop

    def full(self):
        return self.before + 1 + self.loop

    def earlier(self):
        return self.before + self.loop


FIRST = ["xT0", "xT1", "cT0", "cT1", "q0", "k", "q1", "K00", "K01", "K10", "K11", "V", "mT0"]
BODY = ["xT0", "xT1", "cT0", "cT1", "q0", "mT1", "k", "q1", "K00", "K01", "o0", "K10", "mT0", "K11", "V",
        "o1"]
LAST = ["eT", "mT1", "ef0", "ef1", "o0", "o1"]
SPLIT = ["xT0", "xT1", "cT0", "cT1", "q0", "k", "q1"]


def fill_first(name):
    return Fill(FIRST.index(name))


def fill_body(name, i):
    return Fill(len(FIRST) + BODY.index(name), i * (len(BODY) // 2))


def fill_last(name):
    return Fill(len(FIRST) + len(BODY) * (PAIRS - 1) + LAST.index(name))


def flamingo_block(nc, x, ctx, g_attn, g_ffn, Wq, Wk, Wv, Wo, gate_w, up_w, down_w, fc1_w, fc2_w,
                   expert_w, gamma, beta, out):
    stack = ExitStack()
    with stack:
        def sb(name, shape, dt=FP32):
            return stack.enter_context(nc.sbuf_tensor(name, shape, dt))

        def sem(name):
            return stack.enter_context(nc.semaphore(name))

        store = sb("store", [P, 28736], FP32R)
        taken = [0]

        def part(cols, at=None):
            at = taken[0] if at is None else at
            taken[0] = max(taken[0], at + cols)
            return at

        def view(at, *dims):
            n = 1
            for d in dims:
                n *= d
            v = store[:, at:at + n]
            names = "abcde"[:len(dims)]
            if len(dims) > 1:
                v = v.rearrange(f"p ({' '.join(names)}) -> p {' '.join(names)}",
                                **{names[j]: dims[j] for j in range(1, len(dims))})
            return v

        a_wq, a_wk, a_wv = part(2 * KT * D), part(2 * KT * KVD), part(2 * KT * KVD)
        a_xT, a_cT, a_q = part(2 * KT * T), part(2 * KT * T), part(2 * KT * T)
        a_k, a_sel = part(2 * T), part(2 * KV * STACK + 64)
        a_wo, a_oT = part(2 * KT * D), part(2 * KT * T)
        a_qs, a_ks = part(NPAIR * T), part(2 * KV * T)
        wq = view(a_wq, 2, KT, D)
        wk = view(a_wk, 2, KT, KVD)
        wv = view(a_wv, 2, KT, KVD)
        wo = view(a_wo, 2, KT, D)
        xT = view(a_xT, 2, KT, T)
        cT = view(a_cT, 2, KT, T)
        qT = view(a_q, 2, KT, T)
        kT = view(a_k, 2, T)
        sel = view(a_sel, 2, KV, STACK)
        oT = view(a_oT, 2, KT, T)
        qs = view(a_qs, 2, NPAIR, SEQ)
        ks = view(a_ks, 2, KV, 2, SEQ)

        up = view(0, 2, KT, INT)
        fc1 = view(8192, 2, KT, LAT)
        ef = view(10240, 2, LT, D)
        gw = view(12288, KT, 2, NE)
        x2T = view(12352, 2, KT, T)
        hT = view(a_wo, 2, MT, T)
        latT = view(a_oT, 2, LT, T)
        down = view(a_qs, 2, MT, D)

        xall = sb("xall", [P, NSEQ, D])
        ctxb = sb("ctxb", [P, 2, D])
        xn = sb("xn", [P, 2, D])
        probs = sb("probs", [P, 2, 4, 2, T])
        vpad = sb("vpad", [P, 2, KV, 3 * HD])
        onepad = sb("onepad", [P, 3 * HD])
        rden = sb("rden", [P, T])
        onorm = sb("onorm", [P, T])
        raw = sb("raw", [P, 5120])
        raw2 = sb("raw2", [P, 1568])
        raw_down = sb("raw_down", [P, DOWN_EARLY * D])
        expT = sb("expT", [P, LT, LAT])
        over = probs[:, :, :, :, :].rearrange("p u j e t -> p (u j e t)").rearrange("p (n b d) -> p n b d", n=4, b=2)
        relu, hfull, ysum = over[:, 0], over[:, 1], over[:, 2]
        scaled = over[:, 3]
        xg = sb("xg", [P, 2, D])
        gammab = sb("gammab", [P, D])
        betab = sb("betab", [P, D])
        logits = sb("logits", [P, 2, NE])
        top8 = sb("top8", [P, 2, 8])
        rw = sb("rw", [P, 2])
        mv2 = sb("mv2", [P, 2, 2])
        credit = sb("credit", [P, 18])
        st2 = sb("st2", [P, 2, 6])
        vare2 = sb("vare2", [P, 2])
        rstd2 = sb("rstd2", [P, 2])
        nbias2 = sb("nbias2", [P, 2])
        mx = sb("mx", [P, 2, NPAIR, 2])
        negmax = sb("negmax", [P, 2, MAXROWS, NPAIR])
        maxT = sb("maxT", [MAXROWS * NPAIR, 2, P], FP32R)
        ident = sb("ident", [P, P])
        parity = sb("parity", [P, 2])
        maxsel = sb("maxsel", [P, 2])
        stats = sb("stats", [P, NSEQ, 6])
        mv = sb("mv", [P, NSEQ, 2])
        vare = sb("vare", [P, NSEQ])
        rstd = sb("rstd", [P, NSEQ])
        nbias = sb("nbias", [P, NSEQ])
        mhalf = sb("mhalf", [P, NSEQ])
        gates = sb("gates", [P, 2])
        tgates = sb("tgates", [P, 2])

        def bank(name):
            return stack.enter_context(nc.psum_tensor(name, [P, 512], FP32))

        s_bank = [bank("s_bank0"), bank("s_bank1")]
        st_bank = [bank("st_bank0"), bank("st_bank1")]
        o_bank = [bank("o_bank0"), bank("o_bank1")]
        g_bank = [bank("g_bank0"), bank("g_bank1")]

        x0_in, xrest_in, gates_in = sem("x0_in"), sem("xrest_in"), sem("gates_in")
        ctx_in = sem("ctx_in")
        wq_in, wkv_in, wo_in = sem("wq_in"), sem("wkv_in"), sem("wo_in")
        q_stacked = [sem("q_stacked0"), sem("q_stacked1")]
        max_stacked = [sem("max_stacked0"), sem("max_stacked1")]
        stored = sem("stored")
        ident_zero, ident_ready, pool_const = sem("ident_zero"), sem("ident_ready"), sem("pool_const")
        sel_zero, sel_ready = sem("sel_zero"), sem("sel_ready")
        consts = sem("consts")
        wq_hi, wkv_hi, wo_hi = sem("wq_hi"), sem("wkv_hi"), sem("wo_hi")
        wq_lo, wkv_lo, wo_lo = sem("wq_lo"), sem("wkv_lo"), sem("wo_lo")
        var_ready, rstd_ready = sem("var_ready"), sem("rstd_ready")
        nbias_ready = sem("nbias_ready")
        xn_ready = sem("xn_ready")
        tanh_ready = sem("tanh_ready")
        g_full = [sem("g_full0"), sem("g_full1")]
        g_done = [sem("g_done0"), sem("g_done1")]
        g_hi = sem("g_hi")
        s_full, s_free = sem("s_full"), sem("s_free")
        st_full, st_free = sem("st_full"), sem("st_free")
        weighed, o_free = sem("weighed"), sem("o_free")
        rden_ready, oT_hi, oT_lo = sem("rden_ready"), sem("oT_hi"), sem("oT_lo")
        max_split = sem("max_split")
        up_in, small_in, down_in, affine_in = sem("up_in"), sem("small_in"), sem("down_in"), sem("affine_in")
        down_rest_in, up_lo_pool = sem("down_rest_in"), sem("up_lo_pool")
        up_hi, up_lo, down_hi, down_lo = sem("up_hi"), sem("up_lo"), sem("down_hi"), sem("down_lo")
        small_lo = sem("small_lo")
        affine_ready = sem("affine_ready")
        x2n_ready, x2_full, x2_hi, x2_lo = sem("x2n_ready"), sem("x2_full"), sem("x2_hi"), sem("x2_lo")
        up_full, up_free, h_full, h_hi, h_lo = sem("up_full"), sem("up_free"), sem("h_full"), sem("h_hi"), sem("h_lo")
        lat_full, lat_hi, lat_lo, logits_full, rw_ready = (
            sem("lat_full"), sem("lat_hi"), sem("lat_lo"), sem("logits_full"), sem("rw_ready"))
        down_full, y_ready, routed_full, routed_scaled = (
            sem("down_full"), sem("y_ready"), sem("routed_full"), sem("routed_scaled"))
        var2_ready, rstd2_ready, xg_ready, out_ready = (
            sem("var2_ready"), sem("rstd2_ready"), sem("xg_ready"), sem("out_ready"))
        own2 = sem("own2")
        waited = sem("waited")
        own = sem("own")

        def raw_view(t, at, n):
            return t[:, at:at + KT * n].rearrange("p (k n) -> p k n", k=KT)

        def wq_rows(a, k):
            return wq[:, a, k, :].rearrange("p (m r s) -> p m s r", m=KT, s=4)

        def down_raw(k):
            return raw_down[:, k * D:(k + 1) * D] if k < DOWN_EARLY else raw[:, (k - DOWN_EARLY) * D:(k - DOWN_EARLY + 1) * D]

        def wq_raw(k):
            return raw[:, k * D:(k + 1) * D].rearrange("p (s m r) -> p m s r", s=4, m=KT)

        def wait_apart(eng, signal, value):
            eng.wait_ge(signal, value)
            eng.sem_inc(waited, 1)

        block = stack.enter_context(nc.Block())

        @block.sync
        def _(sp):
            x_v = x.rearrange("s t d -> t s d")
            sp.dma_start(xall[:, 0:2, :], x_v[:, 0:2, :]).then_inc(x0_in, 16)
            sp.dma_start(raw[:, 0:2048].rearrange("p (k n) -> p k n", k=KT),
                         Wq.rearrange("(k p) n -> p k n", p=P)).then_inc(wq_in, 16)
            sp.dma_start(ctxb[:, :, :], ctx[0:2].rearrange("s t d -> t s d")).then_inc(ctx_in, 16)
            sp.dma_start(raw[:, 2048:2560].rearrange("p (k n) -> p k n", k=KT),
                         Wk.rearrange("(k p) n -> p k n", p=P)).then_inc(wkv_in, 16)
            sp.dma_start(raw[:, 2560:3072].rearrange("p (k n) -> p k n", k=KT),
                         Wv.rearrange("(k p) n -> p k n", p=P)).then_inc(wkv_in, 16)
            sp.dma_start(xall[:, 2:NSEQ, :], x_v[:, 2:NSEQ, :]).then_inc(xrest_in, 16)
            wo_v = Wo.rearrange("(hh j pp r) n -> hh pp j r n", hh=2, j=4, pp=2)
            for hh in range(2):
                for pp in range(2):
                    kt = 2 * hh + pp
                    sp.dma_start(raw[:, 3072 + kt * D:3072 + (kt + 1) * D], wo_v[hh, pp]).then_inc(wo_in, 16)
            sp.dma_start(gates[:, 0:1], g_attn.rearrange("(a b) -> a b", a=1).to_broadcast([P, 1])).then_inc(gates_in, 16)
            sp.dma_start(gates[:, 1:2], g_ffn.rearrange("(a b) -> a b", a=1).to_broadcast([P, 1])).then_inc(gates_in, 16)

            def load_ctx(i, F):
                f = F("cT1")
                wait_apart(sp, g_full[f.bank], f.full())
                sp.dma_start(ctxb[:, :, :], ctx[bass.ds(2 * i, 2)].rearrange("s t d -> t s d")).then_inc(ctx_in, 16)

            def stack_q(b, F, st_done):
                for name in ("q0", "q1"):
                    f = F(name)
                    wait_apart(sp, g_done[f.bank], f.full())
                if st_done is not None:
                    wait_apart(sp, st_full, st_done)
                for term, src in enumerate((0, 0, 1)):
                    sp.dma_start(qs[2 * HD * term:2 * HD * (term + 1), b, :, :].bitcast(FP32),
                                 qT[:, src, :, b * SEQ:(b + 1) * SEQ].bitcast(FP32)).then_inc(q_stacked[b], 16)

            def stack_max(b, F):
                f = F(f"mT{b}")
                wait_apart(sp, g_done[f.bank], f.full())
                sp.dma_start(qs[STACK:STACK + MAXROWS, b, :, :].bitcast(FP32),
                             maxT[:, b, :].bitcast(FP32)).then_inc(max_stacked[b], 16)

            load_ctx(1, fill_first)
            stack_q(0, fill_first, None)
            stack_q(1, fill_first, None)
            stack_max(0, fill_first)

            sp.wait_ge(wq_lo, KT)
            sp.wait_ge(wkv_lo, 2)
            sp.wait_ge(wo_lo, 1)
            sp.dma_start(raw[:, 0:KT * INT].rearrange("p (k n) -> p k n", k=KT),
                         up_w.rearrange("(k p) n -> p k n", p=P)).then_inc(up_in, 16)
            sp.dma_start(raw[:, KT * INT:KT * (INT + LAT)].rearrange("p (k n) -> p k n", k=KT),
                         fc1_w.rearrange("(k p) n -> p k n", p=P)).then_inc(up_in, 16)
            sp.dma_start(raw2[:, 0:512].rearrange("p (k n) -> p k n", k=LT),
                         expert_w.rearrange("(k p) n -> p k n", p=P)).then_inc(small_in, 16)
            sp.dma_start(raw2[:, 512:1536].rearrange("p (k n) -> p k n", k=LT),
                         fc2_w.rearrange("(k p) n -> p k n", p=P)).then_inc(small_in, 16)
            sp.dma_start(raw2[:, 1536:1568].rearrange("p (k n) -> p k n", k=KT),
                         gate_w.rearrange("(k p) n -> p k n", p=P)).then_inc(small_in, 16)
            sp.dma_start(gammab[:, :], gamma.rearrange("(a b) -> a b", a=1).to_broadcast([P, D])).then_inc(affine_in, 16)
            sp.dma_start(betab[:, :], beta.rearrange("(a b) -> a b", a=1).to_broadcast([P, D])).then_inc(affine_in, 16)

            down_v = down_w.rearrange("(k p) n -> p k n", p=P)
            sp.dma_start(raw_down[:, :].rearrange("p (k n) -> p k n", k=DOWN_EARLY),
                         down_v[:, 0:DOWN_EARLY, :]).then_inc(down_in, 16)

            def body(i, more):
                def F(name):
                    return fill_body(name, i)
                stack_max(1, F)
                stack_q(0, F, 16 * i + 8)
                if more: load_ctx(i + 2, F)
                stack_q(1, F, 16 * i + 16)
                stack_max(0, F)

            with sp.Fori(0, PAIRS - 2) as i:
                body(i, True)
            body(PAIRS - 2, False)
            stack_max(1, fill_last)
            sp.wait_ge(up_lo, 2)
            sp.dma_start(raw[:, 0:(MT - DOWN_EARLY) * D].rearrange("p (k n) -> p k n", k=MT - DOWN_EARLY),
                         down_v[:, DOWN_EARLY:MT, :]).then_inc(down_rest_in, 16)
            with sp.Fori(0, PAIRS) as i:
                wait_apart(sp, out_ready, 2 * i + 2 + 2)
                sp.dma_start(out[bass.ds(2 * i, 2)].rearrange("s t d -> t s d"),
                             xall[:, bass.ds(2 * i, 2), :]).then_inc(stored, 16)
            sp.wait_ge(stored, 16 * PAIRS)

        @block.gpsimd
        def _(pool):
            nc.gpsimd.memset(ident[:, :], 0.0).then_inc(ident_zero, 1)
            pool.wait_ge(ident_zero, 1)
            nc.gpsimd.affine_select(out=ident[:, :], in_=ident[:, :], compare_op=ALU.not_equal, fill=1.0,
                                    base=0, pattern=[[-1, P]], channel_multiplier=1).then_inc(ident_ready, 1)
            nc.gpsimd.memset(mhalf[:, :], -0.5).then_inc(pool_const, 1)
            nc.gpsimd.memset(store[:, a_sel:a_sel + 2 * KV * STACK].bitcast(FP32), 0.0).then_inc(sel_zero, 1)
            nc.gpsimd.memset(onepad[:, :], 0.0).then_inc(pool_const, 1)
            pool.wait_ge(pool_const, 2)
            nc.gpsimd.memset(onepad[:, HD:2 * HD], 1.0).then_inc(pool_const, 1)
            nc.gpsimd.memset(vpad[:, :, :, :], 0.0).then_inc(pool_const, 1)
            pool.wait_ge(var_ready, 1)
            nc.gpsimd.tensor_tensor(rstd[:, 0:2], vare[:, 0:2], mhalf[:, 0:2], ALU.pow).then_inc(rstd_ready, 1)
            for k in (2, 3):
                pool.wait_ge(wq_hi, k)
                nc.gpsimd.tensor_tensor(wq_rows(1, k), wq_raw(k), wq_rows(0, k).bitcast(FP32), ALU.subtract).then_inc(wq_lo, 1)
            pool.wait_ge(var_ready, 2)
            nc.gpsimd.tensor_tensor(rstd[:, 2:NSEQ], vare[:, 2:NSEQ], mhalf[:, 2:NSEQ], ALU.pow).then_inc(rstd_ready, 1)
            pool.wait_ge(wo_in, 64)
            pool.wait_ge(wo_hi, 1)
            nc.gpsimd.tensor_tensor(wo[:, 1], raw_view(raw, 3072, D), wo[:, 0].bitcast(FP32),
                                    ALU.subtract).then_inc(wo_lo, 1)
            pool.wait_ge(affine_in, 32)
            pool.wait_ge(tanh_ready, 1)
            for t in (gammab, betab):
                nc.gpsimd.tensor_scalar(t[:, :], t[:, :], tgates[:, 1:2], None, ALU.mult).then_inc(affine_ready, 1)
            def inverse_std(value):
                pool.wait_ge(var2_ready, value)
                nc.gpsimd.tensor_tensor(rstd2[:, :], vare2[:, :], mhalf[:, 0:2], ALU.pow).then_inc(rstd2_ready, 1)

            def body(i, more):
                pool.wait_ge(affine_ready, 2)
                for b in range(2):
                    pool.wait_ge(out_ready, 2 * i + b + 1)
                    nc.gpsimd.tensor_tensor(xg[:, b:b + 1, :], xall[:, bass.ds(2 * i + b, 1), :],
                                            betab[:, :].unsqueeze(1), ALU.add).then_inc(xg_ready, 1)
                if more:
                    inverse_std(2 * i + 2)
                inverse_std(2 * i + (3 if more else 2))

            inverse_std(1)
            for k in (2, 3):
                pool.wait_ge(up_hi, k + 1)
                nc.gpsimd.tensor_tensor(up[:, 1, k, :], raw[:, k * INT:(k + 1) * INT],
                                        up[:, 0, k, :].bitcast(FP32), ALU.subtract).then_inc(up_lo_pool, 1)
            for k in range(MT // 2, MT):
                pool.wait_ge(down_hi, k + 1)
                nc.gpsimd.tensor_tensor(down[:, 1, k, :], down_raw(k), down[:, 0, k, :].bitcast(FP32),
                                        ALU.subtract).then_inc(down_lo, 1)

            f = fill_last("o1")
            pool.wait_ge(g_done[f.bank], f.full())
            with pool.Fori(0, PAIRS - 1) as i:
                body(i, True)
            body(PAIRS - 1, False)

        @block.scalar
        def _(act):
            def take_hi(name, F, dst, src_cols=512):
                f = F(name)
                act.wait_ge(g_full[f.bank], f.full())
                nc.scalar.activation(dst, g_bank[f.bank][:, 0:src_cols] if len(dst.shape) == 2 else
                                     g_bank[f.bank][:, 0:src_cols].rearrange("p (k t) -> p k t", k=dst.shape[1]),
                                     ACT.Copy).then_inc(g_hi, 1)

            def hi_of(name, F):
                if name[:2] in ("xT", "cT"):
                    b = int(name[2])
                    take_hi(name, F, (xT if name[0] == "x" else cT)[:, 0, :, b * SEQ:(b + 1) * SEQ])
                elif name[0] == "q":
                    m = 2 * int(name[1])
                    take_hi(name, F, qT[:, 0, m:m + 2, :])
                elif name == "k":
                    take_hi(name, F, kT[:, 0, :], T)

            act.wait_ge(ident_ready, 1)
            act.wait_ge(sel_zero, 1)
            id_v = ident[:, :].rearrange("p (h d) -> p h d", h=KV)
            for term, part_ in enumerate((0, 1, 0)):
                for par in range(2):
                    nc.scalar.activation(sel[:, part_, :, (2 * term + par) * HD:(2 * term + par + 1) * HD], id_v,
                                         ACT.Copy).then_inc(sel_ready, 1)
            act.wait_ge(wq_in, 16)
            for k in (0, 2, 3):
                nc.scalar.activation(wq_rows(0, k), wq_raw(k), ACT.Copy).then_inc(wq_hi, 1)
            hi_of("xT0", fill_first)
            hi_of("xT1", fill_first)
            act.wait_ge(wkv_in, 32)
            nc.scalar.activation(wk[:, 0], raw_view(raw, 2048, KVD), ACT.Copy).then_inc(wkv_hi, 1)
            nc.scalar.activation(wv[:, 0], raw_view(raw, 2560, KVD), ACT.Copy).then_inc(wkv_hi, 1)

            def spread_k(b, n, F):
                f = F(f"K{b}{n}")
                act.wait_ge(g_full[f.bank], f.full())
                for par in range(2):
                    last = nc.scalar.activation(
                        ks[0:STACK, b, 4 * n:4 * n + 4, par, :],
                        g_bank[f.bank][0:STACK, :].rearrange("p (h t) -> p h t", h=4),
                        ACT.Copy, scale=parity[0:STACK, par:par + 1])
                last.then_inc(g_done[f.bank], 1)

            def take_v(F):
                f = F("V")
                act.wait_ge(g_full[f.bank], f.full())
                nc.scalar.activation(vpad[:, :, :, HD:2 * HD],
                                     g_bank[f.bank][:, 0:T].rearrange("p (s h d) -> p s h d", s=2, h=KV),
                                     ACT.Copy).then_inc(g_done[f.bank], 1)

            def take_max(b, F):
                f = F(f"mT{b}")
                act.wait_ge(g_full[f.bank], f.full())
                nc.scalar.activation(maxT[:, b, :], g_bank[f.bank][0:MAXROWS * NPAIR, 0:P],
                                     ACT.Copy).then_inc(g_done[f.bank], 1)

            def normalize(i):
                for b in range(2):
                    nc.scalar.activation(xn[:, b:b + 1, :], xall[:, bass.ds(2 * i + b, 1), :], ACT.Identity,
                                         bias=nbias[:, bass.ds(2 * i + b, 1)],
                                         scale=rstd[:, bass.ds(2 * i + b, 1)]).then_inc(xn_ready, 1)

            def exp_step(i, t):
                act.wait_ge(st_full, 16 * i + t + 1)
                g = t // 4
                if t % 4 == 0:
                    act.wait_ge(weighed, 4 * i + g + 1)
                nc.scalar.activation(probs[:, g % 2, t % 4, :, :],
                                     st_bank[t % 2][:, :].rearrange("p (a b) -> p a b", a=2),
                                     ACT.Exp, scale=SCALE).then_inc(st_free, 1)

            for name in SPLIT[2:]:
                hi_of(name, fill_first)
            act.wait_ge(consts, 1)
            for n in range(2):
                spread_k(0, n, fill_first)
            act.wait_ge(wo_in, 64)
            nc.scalar.activation(wo[:, 0], raw_view(raw, 3072, D), ACT.Copy).then_inc(wo_hi, 1)
            act.wait_ge(gates_in, 32)
            nc.scalar.activation(tgates[:, :], gates[:, :], ACT.Tanh).then_inc(tanh_ready, 1)
            for n in range(2):
                spread_k(1, n, fill_first)
            act.wait_ge(pool_const, 4)
            take_v(fill_first)
            take_max(0, fill_first)
            for t in range(4):
                exp_step(0, t)
            act.wait_ge(nbias_ready, 1)
            with act.Fori(0, PAIRS - 1) as i:
                def F(name):
                    return fill_body(name, i)
                normalize(i + 1)
                for t in range(4, 8):
                    exp_step(i, t)
                    hi_of(("xT0", "xT1", "cT0", "cT1")[t - 4], F)
                for b in range(2):
                    act.wait_ge(q_stacked[b], 48 * (i + 1))
                hi_of("q0", F)
                take_max(1, F)
                hi_of("k", F)
                hi_of("q1", F)
                for t in range(8, 16):
                    exp_step(i, t)
                    if t == 10: spread_k(0, 0, F)
                spread_k(1, 0, F)
                take_max(0, F)
                spread_k(1, 1, F)
                take_v(F)
                for t in range(4):
                    exp_step(i + 1, t)
            for t in range(4, 8):
                exp_step(PAIRS - 1, t)
            f = fill_last("eT")
            act.wait_ge(g_full[f.bank], f.full())
            nc.scalar.activation(expT[:, :, :], g_bank[f.bank][:, :].rearrange("p (k n) -> p k n", k=LT),
                                 ACT.Copy).then_inc(g_done[f.bank], 1)
            for name in ("K11", "V"):
                f = fill_body(name, PAIRS - 2)
                act.wait_ge(g_full[f.bank], f.full())
            act.wait_ge(up_in, 32)
            act.wait_ge(small_in, 48)

            def up_hi_part(k):
                nc.scalar.activation(up[:, 0, k, :], raw[:, k * INT:(k + 1) * INT], ACT.Copy).then_inc(up_hi, 1)

            up_hi_part(0)
            take_max(1, fill_last)
            up_hi_part(1)
            for b in range(2):
                act.wait_ge(q_stacked[b], 48 * PAIRS)
            for l in range(LT):
                f = fill_last(f"ef{l}")
                act.wait_ge(g_full[f.bank], f.full())
                nc.scalar.activation(ef[:, 0, l, :], g_bank[f.bank][:, :], ACT.Copy).then_inc(g_hi, 1)
            for t in range(8, 16):
                exp_step(PAIRS - 1, t)
            up_hi_part(2)
            up_hi_part(3)
            nc.scalar.activation(fc1[:, 0], raw_view(raw, KT * INT, LAT), ACT.Copy)
            nc.scalar.activation(gw[:, :, 0, :], raw_view(raw2, 1536, NE), ACT.Copy).then_inc(up_hi, 1)

            def x2_hi_part(i, b):
                act.wait_ge(x2_full, 2 * i + b + 1)
                nc.scalar.activation(x2T[:, 0, :, b * SEQ:(b + 1) * SEQ],
                                     st_bank[b][:, :].rearrange("p (k t) -> p k t", k=KT), ACT.Copy).then_inc(x2_hi, 1)

            for b in range(2):
                x2_hi_part(0, b)
            act.wait_ge(down_in, 16)
            act.wait_ge(st_full, 16 * PAIRS)
            for k in range(MT):
                if k == DOWN_EARLY: act.wait_ge(down_rest_in, 16)
                nc.scalar.activation(down[:, 0, k, :], down_raw(k), ACT.Copy).then_inc(down_hi, 1)

            def ffn(i, more):
                for u in range(MT // 2):
                    act.wait_ge(up_full, 4 * i + u + 1)
                    nc.scalar.activation(relu[:, u % 2, :], s_bank[u % 2][:, :], ACT.Relu).then_inc(up_free, 1)
                    act.wait_ge(up_free, 4 * i + u + 1 + 2)
                    act.wait_ge(h_lo, 4 * i + u + 1)
                    nc.scalar.activation(hfull[:, u % 2, :], relu[:, u % 2, :], ACT.Square).then_inc(h_full, 1)
                act.wait_ge(lat_full, i + 1)
                nc.scalar.activation(latT[:, 0], o_bank[0][:, :].rearrange("p (k t) -> p k t", k=LT),
                                     ACT.Copy).then_inc(lat_hi, 1)
                if more:
                    for b in range(2):
                        x2_hi_part(i + 1, b)
                for b in range(2):
                    act.wait_ge(routed_full, 2 * i + b + 1)
                    act.wait_ge(rw_ready, i + 1)
                    act.wait_ge(y_ready, 2 * i + b + 1)
                    nc.scalar.activation(scaled[:, b, :], o_bank[b][:, :], ACT.Copy,
                                         scale=rw[:, b:b + 1]).then_inc(routed_scaled, 1)

            with act.Fori(0, PAIRS - 1) as i:
                ffn(i, True)
            ffn(PAIRS - 1, False)

        @block.vector
        def _(dve):
            count = [0]

            def mine(ins):
                count[0] += 1
                ins.then_inc(own, 1)
                dve.wait_ge(own, count[0])

            for n, free in enumerate((s_free, st_free, o_free, weighed, up_free, h_lo, y_ready, routed_scaled, out_ready)):
                for m in range(2):
                    nc.vector.memset(credit[:, 2 * n + m:2 * n + m + 1], 0.0).then_inc(free, 1)

            def ln_stats(lo, hi):
                for s in range(lo, hi):
                    last = nc.vector.bn_stats(stats[:, s, :], xall[:, s, :])
                mine(last)
                for s in range(lo, hi):
                    last = nc.vector.bn_aggr(mv[:, s, :], stats[:, s, :])
                mine(last)
                nc.vector.tensor_scalar(vare[:, lo:hi], mv[:, lo:hi, 1], EPS, None, ALU.add).then_inc(var_ready, 1)

            def ln_bias(lo, hi, which):
                dve.wait_ge(rstd_ready, which)
                mine(nc.vector.scalar_tensor_tensor(out=nbias[:, lo:hi], in0=mv[:, lo:hi, 0], scalar=-1.0,
                                                    in1=rstd[:, lo:hi], op0=ALU.mult, op1=ALU.mult))

            def normalize(i):
                for b in range(2):
                    nc.vector.tensor_scalar(xn[:, b:b + 1, :], xall[:, bass.ds(2 * i + b, 1), :],
                                            rstd_col(rstd, i, b), rstd_col(nbias, i, b),
                                            ALU.mult, ALU.add).then_inc(xn_ready, 1)

            def rstd_col(t, i, b):
                return t[:, bass.ds(2 * i + b, 1)]

            def take_lo(name, F, a):
                f = F(name)
                dve.wait_ge(g_hi, len(SPLIT) * a + SPLIT.index(name) + 1)
                if name[:2] in ("xT", "cT"):
                    b = int(name[2])
                    t = xT if name[0] == "x" else cT
                    dst, hi = t[:, 1, :, b * SEQ:(b + 1) * SEQ], t[:, 0, :, b * SEQ:(b + 1) * SEQ]
                    src = g_bank[f.bank][:, :].rearrange("p (k t) -> p k t", k=KT)
                elif name[0] == "q":
                    m = 2 * int(name[1])
                    dst, hi = qT[:, 1, m:m + 2, :], qT[:, 0, m:m + 2, :]
                    src = g_bank[f.bank][:, :].rearrange("p (k t) -> p k t", k=2)
                else:
                    dst, hi, src = kT[:, 1, :], kT[:, 0, :], g_bank[f.bank][:, 0:T]
                nc.vector.tensor_tensor(dst, src, hi.bitcast(FP32), ALU.subtract).then_inc(g_done[f.bank], 1)

            def spread_k(b, n, F):
                f = F(f"K{b}{n}")
                dve.wait_ge(g_full[f.bank], f.full())
                for par in range(2):
                    last = nc.vector.tensor_scalar(
                        ks[0:STACK, b, 4 * n:4 * n + 4, par, :],
                        g_bank[f.bank][0:STACK, :].rearrange("p (h t) -> p h t", h=4),
                        parity[0:STACK, par:par + 1], None, ALU.mult)
                last.then_inc(g_done[f.bank], 1)

            def row_max(i, s):
                dve.wait_ge(s_full, 16 * i + s + 1)
                b, h = s // 8, s % 8
                nc.vector.reduce_max(mx[:, b, 2 * h:2 * h + 2, :],
                                     s_bank[s % 2][:, :].rearrange("p (a e k) -> p a e k", a=2, e=2),
                                     AX.X).then_inc(s_free, 1)

            def split_max(i, b):
                dve.wait_ge(s_free, 16 * i + 8 * b + 8 + 2)
                v = negmax[:, b].rearrange("p (e l) n -> p e l n", e=2)
                m = mx[:, b].rearrange("p n e -> p e n")
                nc.vector.tensor_scalar(v[:, :, 0, :].bitcast(FP32R), m, -1.0, None, ALU.mult).then_inc(max_split, 1)
                dve.wait_ge(max_split, 4 * i + 2 * b + 1)
                nc.vector.scalar_tensor_tensor(out=v[:, :, 1, :].bitcast(FP32R), in0=m, scalar=-1.0,
                                               in1=v[:, :, 0, :], op0=ALU.mult, op1=ALU.subtract).then_inc(max_split, 1)

            def head_outputs(i, g):
                b, hh = g // 2, g % 2
                bank = o_bank[g % 2]
                dve.wait_ge(weighed, 4 * i + g + 1 + 2)
                nc.vector.reciprocal(rden[:, :], bank[:, T:2 * T]).then_inc(rden_ready, 1)
                dve.wait_ge(rden_ready, 4 * i + g + 1)
                nc.vector.tensor_tensor(onorm[:, :], bank[:, 0:T], rden[:, :], ALU.mult).then_inc(o_free, 1)
                dve.wait_ge(o_free, 4 * i + g + 1 + 2)
                on = onorm[:, :].rearrange("p (k t) -> p k t", k=2)
                hi = oT[:, 0, 2 * hh:2 * hh + 2, b * SEQ:(b + 1) * SEQ]
                nc.vector.tensor_copy(hi, on).then_inc(oT_hi, 1)
                dve.wait_ge(oT_hi, 4 * i + g + 1)
                nc.vector.tensor_tensor(oT[:, 1, 2 * hh:2 * hh + 2, b * SEQ:(b + 1) * SEQ], on,
                                        hi.bitcast(FP32), ALU.subtract).then_inc(oT_lo, 1)

            def add_attention(i, b, F):
                f = F(f"o{b}")
                dve.wait_ge(g_full[f.bank], f.full())
                xb = xall[:, bass.ds(2 * i + b, 1), :].rearrange("p a d -> p (a d)")
                nc.vector.scalar_tensor_tensor(out=xb, in0=g_bank[f.bank][:, :], scalar=tgates[:, 0:1], in1=xb,
                                               op0=ALU.mult, op1=ALU.add).then_inc(g_done[f.bank], 1)

            dve.wait_ge(ident_ready, 1)
            for par in range(2):
                nc.vector.reduce_sum(parity[:, par:par + 1],
                                     ident[:, :].rearrange("p (a e d) -> p e a d", e=2, d=HD)[:, par],
                                     AX.XY)
                last = nc.vector.reduce_sum(maxsel[:, par:par + 1],
                                            ident[:, STACK + 2 * par:STACK + 2 * par + 2], AX.X)
            mine(last)
            for par in range(2):
                last = nc.vector.tensor_scalar(
                    ks[STACK:P, :, :, par, :].rearrange("p s h t -> p (s h) t"),
                    ident[STACK:P, 0:1].unsqueeze(2).to_broadcast([32, 2 * KV, SEQ]), 0.0,
                    maxsel[STACK:P, par:par + 1], ALU.mult, ALU.add)
            last.then_inc(consts, 1)
            dve.wait_ge(x0_in, 16)
            ln_stats(0, 2)
            ln_bias(0, 2, 1)
            normalize(0)
            dve.wait_ge(wq_in, 16)
            mine(nc.vector.tensor_copy(wq_rows(0, 1), wq_raw(1)))
            dve.wait_ge(wq_hi, 1)
            for k in (1, 0):
                nc.vector.tensor_tensor(wq_rows(1, k), wq_raw(k), wq_rows(0, k).bitcast(FP32), ALU.subtract).then_inc(wq_lo, 1)
            take_lo("xT0", fill_first, 0)
            take_lo("xT1", fill_first, 0)
            take_lo("cT0", fill_first, 0)
            take_lo("cT1", fill_first, 0)
            dve.wait_ge(wkv_hi, 2)
            nc.vector.tensor_tensor(wk[:, 1], raw_view(raw, 2048, KVD), wk[:, 0].bitcast(FP32), ALU.subtract).then_inc(wkv_lo, 1)
            nc.vector.tensor_tensor(wv[:, 1], raw_view(raw, 2560, KVD), wv[:, 0].bitcast(FP32), ALU.subtract).then_inc(wkv_lo, 1)
            for name in SPLIT[4:]:
                take_lo(name, fill_first, 0)
            dve.wait_ge(xrest_in, 16)
            ln_stats(2, NSEQ)
            for s in range(8):
                row_max(0, s)
            split_max(0, 0)
            ln_bias(2, NSEQ, 2)
            nc.vector.memset(credit[:, 0:1], 0.0).then_inc(nbias_ready, 1)
            dve.wait_ge(tanh_ready, 1)
            for s in range(8, 12):
                row_max(0, s)
            with dve.Fori(0, PAIRS - 1) as i:
                def F(name):
                    return fill_body(name, i)
                for s in range(12, 16):
                    row_max(i, s)
                    take_lo(("xT0", "xT1", "cT0", "cT1")[s - 12], F, i + 1)
                split_max(i, 1)
                take_lo("q0", F, i + 1)
                head_outputs(i, 0)
                take_lo("k", F, i + 1)
                head_outputs(i, 1)
                take_lo("q1", F, i + 1)
                spread_k(0, 1, F)
                for s in range(8):
                    row_max(i + 1, s)
                    if s == 3: add_attention(i, 0, F)
                split_max(i + 1, 0)
                head_outputs(i, 2)
                head_outputs(i, 3)
                row_max(i + 1, 8)
                row_max(i + 1, 9)
                row_max(i + 1, 10)
                row_max(i + 1, 11)
                add_attention(i, 1, F)

            seen = [0]

            def chained(ins, i):
                seen[0] += 1
                ins.then_inc(own2, 1)
                wait_apart(dve, own2, OWN2 * i + seen[0])

            def inverse_std(src, i, which):
                for b in range(2):
                    last = nc.vector.bn_stats(st2[:, b, :], src(b))
                chained(last, i)
                for b in range(2):
                    last = nc.vector.bn_aggr(mv2[:, b, :], st2[:, b, :])
                chained(last, i)
                nc.vector.tensor_scalar(vare2[:, :], mv2[:, :, 1], EPS, None, ALU.add).then_inc(var2_ready, 1)
                dve.wait_ge(rstd2_ready, which)

            def normalize2(i, which, a):
                inverse_std(lambda b: xall[:, bass.ds(2 * a + b, 1), :].rearrange("p a d -> p (a d)"), i, which)
                chained(nc.vector.scalar_tensor_tensor(out=nbias2[:, :], in0=mv2[:, :, 0], scalar=-1.0,
                                                       in1=rstd2[:, :], op0=ALU.mult, op1=ALU.mult), i)
                for b in range(2):
                    nc.vector.tensor_scalar(xn[:, b:b + 1, :], xall[:, bass.ds(2 * a + b, 1), :],
                                            rstd2[:, b:b + 1], nbias2[:, b:b + 1],
                                            ALU.mult, ALU.add).then_inc(x2n_ready, 1)

            def x2_lo_part(i, b):
                dve.wait_ge(x2_hi, 2 * i + b + 1)
                nc.vector.tensor_tensor(x2T[:, 1, :, b * SEQ:(b + 1) * SEQ],
                                        st_bank[b][:, :].rearrange("p (k t) -> p k t", k=KT),
                                        x2T[:, 0, :, b * SEQ:(b + 1) * SEQ].bitcast(FP32),
                                        ALU.subtract).then_inc(x2_lo, 1)

            for s in range(12, 16):
                row_max(PAIRS - 1, s)
            split_max(PAIRS - 1, 1)
            normalize2(0, 1, 0)
            head_outputs(PAIRS - 1, 0)
            head_outputs(PAIRS - 1, 1)

            def up_lo_part(k):
                dve.wait_ge(up_hi, k + 1)
                nc.vector.tensor_tensor(up[:, 1, k, :], raw[:, k * INT:(k + 1) * INT],
                                        up[:, 0, k, :].bitcast(FP32), ALU.subtract).then_inc(up_lo, 1)

            for l in range(LT):
                f = fill_last(f"ef{l}")
                dve.wait_ge(g_hi, len(SPLIT) * PAIRS + l + 1)
                nc.vector.tensor_tensor(ef[:, 1, l, :], g_bank[f.bank][:, :], ef[:, 0, l, :].bitcast(FP32),
                                        ALU.subtract).then_inc(g_done[f.bank], 1)
            up_lo_part(0)
            up_lo_part(1)
            head_outputs(PAIRS - 1, 2)
            head_outputs(PAIRS - 1, 3)
            for b in range(2):
                x2_lo_part(0, b)
            dve.wait_ge(up_hi, 5)
            nc.vector.tensor_tensor(gw[:, :, 1, :], raw_view(raw2, 1536, NE), gw[:, :, 0, :].bitcast(FP32),
                                    ALU.subtract).then_inc(small_lo, 1)
            nc.vector.tensor_tensor(fc1[:, 1], raw_view(raw, KT * INT, LAT), fc1[:, 0].bitcast(FP32),
                                    ALU.subtract).then_inc(up_lo, 1)
            for k in range(MT // 2):
                dve.wait_ge(down_hi, k + 1)
                nc.vector.tensor_tensor(down[:, 1, k, :], down_raw(k), down[:, 0, k, :].bitcast(FP32),
                                        ALU.subtract).then_inc(down_lo, 1)
            for b in range(2):
                add_attention(PAIRS - 1, b, fill_last)

            start2 = seen[0]

            def ffn(i, more):
                seen[0] = start2
                if more:
                    normalize2(i, 2 * i + 2, i + 1)
                for u in range(MT // 2):
                    dve.wait_ge(h_full, 4 * i + u + 1)
                    src = hfull[:, u % 2, :].rearrange("p (m t) -> p m t", m=2)
                    nc.vector.tensor_copy(hT[:, 0, 2 * u:2 * u + 2, :], src).then_inc(h_hi, 1)
                    dve.wait_ge(h_hi, 4 * i + u + 1)
                    nc.vector.tensor_tensor(hT[:, 1, 2 * u:2 * u + 2, :], src,
                                            hT[:, 0, 2 * u:2 * u + 2, :].bitcast(FP32), ALU.subtract).then_inc(h_lo, 1)
                dve.wait_ge(lat_hi, i + 1)
                nc.vector.tensor_tensor(latT[:, 1], o_bank[0][:, :].rearrange("p (k t) -> p k t", k=LT),
                                        latT[:, 0].bitcast(FP32), ALU.subtract).then_inc(lat_lo, 1)
                wait_apart(dve, logits_full, i + 1)
                both = o_bank[1][:, 0:4 * NE].rearrange("p (b h e) -> p b h e", b=2, h=2)
                chained(nc.vector.tensor_copy(logits[:, :, :], both[:, :, 1, :]), i)
                chained(nc.vector.tensor_tensor(logits[:, :, :], both[:, :, 0, :], logits[:, :, :], ALU.add), i)
                for b in range(2):
                    last = nc.vector.max(top8[:, b, :], logits[:, b, :])
                chained(last, i)
                nc.vector.tensor_tensor(rw[:, :], top8[:, :, 0], top8[:, :, 1], ALU.add).then_inc(rw_ready, 1)
                if more:
                    for b in range(2):
                        x2_lo_part(i + 1, b)
                for b in range(2):
                    dve.wait_ge(down_full, 2 * i + b + 1)
                    dve.wait_ge(routed_scaled, 2 * i + b + 1 + 2)
                    nc.vector.tensor_tensor(ysum[:, b, :], g_bank[b][:, :], scaled[:, b, :], ALU.add).then_inc(y_ready, 1)
                dve.wait_ge(y_ready, 2 * i + 2 + 2)
                inverse_std(lambda b: ysum[:, b, :], i, 2 * i + (3 if more else 2))
                dve.wait_ge(affine_ready, 2)
                for b in range(2):
                    last = nc.vector.scalar_tensor_tensor(out=ysum[:, b, :], in0=ysum[:, b, :], scalar=mv2[:, b, 0:1],
                                                          in1=gammab[:, :], op0=ALU.subtract, op1=ALU.mult)
                chained(last, i)
                dve.wait_ge(xg_ready, 2 * i + 2)
                for b in range(2):
                    nc.vector.scalar_tensor_tensor(out=xall[:, bass.ds(2 * i + b, 1), :].rearrange("p a d -> p (a d)"),
                                                   in0=ysum[:, b, :], scalar=rstd2[:, b:b + 1], in1=xg[:, b, :],
                                                   op0=ALU.mult, op1=ALU.add).then_inc(out_ready, 1)

            with dve.Fori(0, PAIRS - 1) as i:
                ffn(i, True)
                assert seen[0] == start2 + OWN2
            ffn(PAIRS - 1, False)

        @block.tensor
        def _(pe):
            def keep_warm(n):
                for _ in range(n):
                    nc.tensor.matmul(o_bank[0][:, 0:P], ident[:, :], ident[:, :], start=True, stop=True)

            def claim(name, F):
                f = F(name)
                if not (isinstance(f.earlier(), int) and f.earlier() == 0):
                    pe.wait_ge(g_done[f.bank], f.earlier())
                return f

            def ready(name, F):
                f = F(name)
                pe.wait_ge(g_done[f.bank], f.full())

            def transposed(name, F, src):
                f = claim(name, F)
                for k in range(KT):
                    last = nc.tensor.transpose(g_bank[f.bank][:, k * P:(k + 1) * P], src[:, k * P:(k + 1) * P],
                                               ident[:, :])
                last.then_inc(g_full[f.bank], 1)

            def three(dst, lhs, rhs, tiles):
                n = 0
                for k in range(tiles):
                    for a, c in ((0, 0), (0, 1), (1, 0)):
                        last = nc.tensor.matmul(dst, lhs(a, k), rhs(c, k), start=(n == 0), stop=(n == 3 * tiles - 1))
                        n += 1
                return last

            def project_q_tile(m, F):
                f = F(f"q{m // 2}")
                last = three(g_bank[f.bank][:, m % 2 * T:(m % 2 + 1) * T], lambda a, k: wq[:, a, k, m * P:(m + 1) * P],
                             lambda c, k: xT[:, c, k, :], KT)
                if m % 2: last.then_inc(g_full[f.bank], 1)

            def project_k(F):
                f = claim("k", F)
                three(g_bank[f.bank][:, 0:T], lambda a, k: wk[:, a, k, :], lambda c, k: cT[:, c, k, :],
                      KT).then_inc(g_full[f.bank], 1)

            def project_v(F):
                f = claim("V", F)
                for b in range(2):
                    last = three(g_bank[f.bank][:, b * KVD:(b + 1) * KVD],
                                 lambda a, k: cT[:, a, k, b * SEQ:(b + 1) * SEQ], lambda c, k: wv[:, c, k, :], KT)
                last.then_inc(g_full[f.bank], 1)

            def select_k(b, n, F):
                f = claim(f"K{b}{n}", F)
                for h in range(4):
                    dst = g_bank[f.bank][0:STACK, h * SEQ:(h + 1) * SEQ]
                    nc.tensor.matmul(dst, sel[:, 0, 4 * n + h, :], kT[:, 0, b * SEQ:(b + 1) * SEQ], start=True, stop=False)
                    last = nc.tensor.matmul(dst, sel[:, 1, 4 * n + h, :], kT[:, 1, b * SEQ:(b + 1) * SEQ],
                                            start=False, stop=True)
                last.then_inc(g_full[f.bank], 1)

            def scores(i, s):
                b, h = s // 8, s % 8
                if h == 0:
                    pe.wait_ge(q_stacked[b], 48 * (i + 1))
                pe.wait_ge(s_free, 16 * i + s + 1)
                for p in range(2):
                    last = nc.tensor.matmul(s_bank[s % 2][:, p * T:(p + 1) * T], qs[0:STACK, b, 2 * h + p, :],
                                            ks[0:STACK, b, h, :, :], start=True, stop=True)
                last.then_inc(s_full, 1)

            def transpose_max(i, b, F):
                f = claim(f"mT{b}", F)
                wait_apart(pe, max_split, 4 * i + 2 * b + 2)
                nc.tensor.transpose(g_bank[f.bank][0:MAXROWS * NPAIR, 0:P],
                                    negmax[:, b].rearrange("p r n -> p (r n)"), ident[:, :]).then_inc(g_full[f.bank], 1)

            def scores_t(i, t):
                b, h = t // 8, t % 8
                if h == 0:
                    pe.wait_ge(max_stacked[b], 16 * (i + 1))
                pe.wait_ge(st_free, 16 * i + t + 1)
                for par in range(2):
                    last = nc.tensor.matmul(st_bank[t % 2][:, par * T:(par + 1) * T],
                                            ks[0:STACK + MAXROWS, b, h, par, :],
                                            qs[0:STACK + MAXROWS, b, 2 * h:2 * h + 2, :], start=True, stop=True)
                last.then_inc(st_full, 1)

            def weigh_values(i, g, parts=(0, 1)):
                b, hh = g // 2, g % 2
                bank = o_bank[g % 2]
                if 0 in parts:
                    pe.wait_ge(st_free, 16 * i + 4 * g + 4 + 2)
                    pe.wait_ge(o_free, 4 * i + g + 1)
                for what in parts:
                    for par in range(2):
                        for j in range(4):
                            lo = HD * (1 - par)
                            w = vpad[:, b, 4 * hh + j, lo:lo + 2 * HD] if what == 0 else onepad[:, lo:lo + 2 * HD]
                            last = nc.tensor.matmul(bank[32 * j:32 * j + 32, what * T:(what + 1) * T], w,
                                                    probs[:, g % 2, j, par, :], start=(par == 0), stop=(par == 1),
                                                    tile_position=(0, 32 * j))
                if 1 in parts: last.then_inc(weighed, 1)

            def project_out(i, b, F):
                f = claim(f"o{b}", F)
                pe.wait_ge(oT_lo, 4 * i + 2 * b + 2)
                three(g_bank[f.bank][:, :], lambda a, k: oT[:, a, k, b * SEQ:(b + 1) * SEQ],
                      lambda c, k: wo[:, c, k, :], KT).then_inc(g_full[f.bank], 1)

            pe.wait_ge(ident_ready, 1)
            keep_warm(WARM_START)
            for b in range(2):
                pe.wait_ge(xn_ready, b + 1)
                transposed(f"xT{b}", fill_first, xn[:, b, :])
            pe.wait_ge(ctx_in, 16)
            for b in range(2):
                transposed(f"cT{b}", fill_first, ctxb[:, b, :])
            ready("xT0", fill_first)
            ready("xT1", fill_first)
            pe.wait_ge(wq_lo, KT)
            for m in range(KT):
                if m % 2 == 0: claim(f"q{m // 2}", fill_first)
                project_q_tile(m, fill_first)
                if m == 1:
                    ready("cT0", fill_first)
                    ready("cT1", fill_first)
                    pe.wait_ge(wkv_lo, 2)
                    project_k(fill_first)
            ready("k", fill_first)
            pe.wait_ge(sel_ready, 2 * 3)
            pe.wait_ge(consts, 1)
            for n in range(2):
                select_k(0, n, fill_first)
            keep_warm(WARM_STACK)
            for n in range(2):
                ready(f"K0{n}", fill_first)
            for s in range(8):
                scores(0, s)
                if s == 1: select_k(1, 0, fill_first)
                if s == 2: select_k(1, 1, fill_first)
                if s == 4: project_v(fill_first)
            transpose_max(0, 0, fill_first)
            keep_warm(WARM_MAX)
            for n in range(2):
                ready(f"K1{n}", fill_first)
            pe.wait_ge(pool_const, 4)
            for t in range(4):
                scores_t(0, t)
                scores(0, 8 + t)
            with pe.Fori(0, PAIRS - 1) as i:
                def F(name):
                    return fill_body(name, i)
                for t in range(4, 8):
                    scores_t(i, t)
                    scores(i, 8 + t)
                    if t == 4:
                        pe.wait_ge(xn_ready, 2 * i + 3)
                        transposed("xT0", F, xn[:, 0, :])
                    if t == 5:
                        pe.wait_ge(xn_ready, 2 * i + 4)
                        transposed("xT1", F, xn[:, 1, :])
                        weigh_values(i, 0, (0,))
                    if t == 6:
                        weigh_values(i, 0, (1,))
                        pe.wait_ge(ctx_in, 16 * i + 32)
                        transposed("cT0", F, ctxb[:, 0, :])
                    if t == 7: transposed("cT1", F, ctxb[:, 1, :])
                ready("xT0", F)
                ready("xT1", F)
                claim("q0", F)
                project_q_tile(0, F)
                project_q_tile(1, F)
                transpose_max(i, 1, F)
                weigh_values(i, 1)
                ready("cT0", F)
                ready("cT1", F)
                project_k(F)
                claim("q1", F)
                project_q_tile(2, F)
                project_q_tile(3, F)
                for t in range(8, 16):
                    scores_t(i, t)
                    if t == 9:
                        ready("k", F)
                        select_k(0, 0, F)
                    if t == 10: select_k(0, 1, F)
                    if t == 11:
                        pe.wait_ge(wo_lo, 1)
                        project_out(i, 0, F)
                        for n in range(2):
                            ready(f"K0{n}", F)
                    if t >= 12: scores(i + 1, t - 12)
                    if t == 13: weigh_values(i, 2, (0,))
                    if t == 14: weigh_values(i, 2, (1,))
                for s in range(4, 8):
                    scores(i + 1, s)
                    if s == 4: weigh_values(i, 3, (0,))
                    if s == 5: weigh_values(i, 3, (1,))
                select_k(1, 0, F)
                transpose_max(i + 1, 0, F)
                select_k(1, 1, F)
                project_v(F)
                for t in range(4):
                    scores_t(i + 1, t)
                    if t == 1:
                        for n in range(2):
                            ready(f"K1{n}", F)
                        scores(i + 1, 8)
                    if t == 2: scores(i + 1, 9)
                project_out(i, 1, F)
                scores(i + 1, 10)
                scores(i + 1, 11)
            last_pair = PAIRS - 1

            def transpose_x2(i, b):
                pe.wait_ge(x2n_ready, 2 * i + b + 1)
                for k in range(KT):
                    last = nc.tensor.transpose(st_bank[b][:, k * P:(k + 1) * P], xn[:, b, k * P:(k + 1) * P], ident[:, :])
                last.then_inc(x2_full, 1)

            for t in range(4, 8):
                scores_t(last_pair, t)
                scores(last_pair, 8 + t)
                if t == 4:
                    f = claim("eT", fill_last)
                    pe.wait_ge(small_in, 48)
                    for m in range(LT):
                        for l in range(LT):
                            last = nc.tensor.transpose(g_bank[f.bank][:, (2 * m + l) * P:(2 * m + l + 1) * P],
                                                       raw2[:, l * LAT + m * P:l * LAT + (m + 1) * P], ident[:, :])
                    last.then_inc(g_full[f.bank], 1)
                if t == 5: weigh_values(last_pair, 0)
            transpose_max(last_pair, 1, fill_last)
            weigh_values(last_pair, 1)
            ready("eT", fill_last)
            for l in range(LT):
                f = claim(f"ef{l}", fill_last)
                for m in range(LT):
                    last = nc.tensor.matmul(g_bank[f.bank][:, :], expT[:, m, l * P:(l + 1) * P],
                                            raw2[:, 512 + m * D:512 + (m + 1) * D],
                                            start=(m == 0), stop=(m == LT - 1))
                last.then_inc(g_full[f.bank], 1)
            for t in range(8, 16):
                scores_t(last_pair, t)
                if t == 13: weigh_values(last_pair, 2)
            weigh_values(last_pair, 3)
            project_out(last_pair, 0, fill_last)
            pe.wait_ge(st_free, 16 * PAIRS + 2)
            for b in range(2):
                transpose_x2(0, b)
            project_out(last_pair, 1, fill_last)

            pe.wait_ge(s_free, 16 * PAIRS + 2)
            pe.wait_ge(o_free, 4 * PAIRS + 2)
            pe.wait_ge(up_lo, 3)
            pe.wait_ge(up_lo_pool, 2)
            pe.wait_ge(small_lo, 1)
            ready("ef0", fill_last)
            ready("ef1", fill_last)

            def ffn(i, more):
                pe.wait_ge(x2_lo, 2 * i + 2)
                for u in range(MT // 2):
                    pe.wait_ge(up_free, 4 * i + u + 1)
                    for m in range(2):
                        cols = (2 * u + m) * P
                        last = three(s_bank[u % 2][:, m * T:(m + 1) * T], lambda a, k: up[:, a, k, cols:cols + P],
                                     lambda c, k: x2T[:, c, k, :], KT)
                    last.then_inc(up_full, 1)
                pe.wait_ge(routed_scaled, 2 * i + 2)
                for m in range(LT):
                    last = three(o_bank[0][:, m * T:(m + 1) * T], lambda a, k: fc1[:, a, k, m * P:(m + 1) * P],
                                 lambda c, k: x2T[:, c, k, :], KT)
                last.then_inc(lat_full, 1)
                for b in range(2):
                    at = 2 * NE * b
                    for k in range(KT):
                        nc.tensor.matmul(o_bank[1][:, at:at + 2 * NE], x2T[:, 0, k, b * SEQ:(b + 1) * SEQ],
                                         gw[:, k, :, :], start=(k == 0), stop=False)
                    for k in range(KT):
                        last = nc.tensor.matmul(o_bank[1][:, at:at + NE], x2T[:, 1, k, b * SEQ:(b + 1) * SEQ],
                                                gw[:, k, 0, :], start=False, stop=(k == KT - 1))
                last.then_inc(logits_full, 1)
                if more:
                    for b in range(2):
                        transpose_x2(i + 1, b)
                pe.wait_ge(down_lo, MT)
                pe.wait_ge(h_lo, 4 * i + 4 + 2)
                for b in range(2):
                    pe.wait_ge(y_ready, 2 * i + b + 1)
                    three(g_bank[b][:, :], lambda a, k: hT[:, a, k, b * SEQ:(b + 1) * SEQ],
                          lambda c, k: down[:, c, k, :], MT).then_inc(down_full, 1)
                pe.wait_ge(lat_lo, i + 1)
                pe.wait_ge(rw_ready, i + 1)
                for b in range(2):
                    three(o_bank[b][:, :], lambda a, k: latT[:, a, k, b * SEQ:(b + 1) * SEQ],
                          lambda c, k: ef[:, c, k, :], LT).then_inc(routed_full, 1)

            with pe.Fori(0, PAIRS - 1) as i:
                ffn(i, True)
            ffn(PAIRS - 1, False)


_INS = ['x', 'ctx_4096', 'g_xattn', 'g_ffn', 'L0_xattn_Wq', 'L0_xattn_Wk', 'L0_xattn_Wv', 'L0_xattn_Wo',
        'L0_ffn_gate_w', 'L0_ffn_up_w', 'L0_ffn_down_w', 'L0_ffn_fc1_w', 'L0_ffn_fc2_w', 'L0_ffn_expert_w',
        'L0_ffn_ln_gamma', 'L0_ffn_ln_beta']
_OUT = ((8, 128, 512), 'float32')


def kernel(**inputs):
    import numpy as _np
    import concourse.bacc as _bacc
    from concourse.bass_utils import run_bass_kernel_spmd as _run

    nc = _bacc.Bacc("TRN2", target_bir_lowering=False, num_devices=1)
    arrays, args = {}, []
    for name in _INS:
        a = _np.ascontiguousarray(inputs[name])
        arrays[f"in_{name}_dram"] = a
        args.append(nc.dram_tensor(f"in_{name}_dram", a.shape, mybir.dt.from_np(a.dtype), kind="ExternalInput").ap())
    args.append(nc.dram_tensor("out_0_dram", _OUT[0], mybir.dt.from_np(_np.dtype(_OUT[1])), kind="ExternalOutput").ap())
    flamingo_block(nc, *args)
    r = _run(nc, [arrays], core_ids=[0])
    return r.results[0]["out_0_dram"]
```

```python
from contextlib import ExitStack

import concourse.bass as bass
from concourse import mybir

FP32 = mybir.dt.float32
FP32R = mybir.dt.float32r
ALU = mybir.AluOpType
ACT = mybir.ActivationFunctionType
AX = mybir.AxisListType

P = 128
NSEQ = 8
SEQ = 128
D = 512
KT = D // P
HEADS, KV, HD = 32, 8, 16
GROUP = HEADS // KV
NPAIR = HEADS // 2
PAIRS = NSEQ // 2
T = 2 * SEQ
KVD = KV * HD
INT, LAT, NE = 1024, 256, 8
MT = INT // P
LT = LAT // P
STACK = 3 * 2 * HD
MAXROWS = 4
DOWN_EARLY = 5
OWN2 = 9
SCALE = float(HD) ** -0.5
EPS = 1e-5


WARM_START, WARM_SPLIT, WARM_STACK, WARM_MAX, WARM_LOOP = 14, 8, 14, 12, 4


class Fill:

    def __init__(self, number, loop=0):
        self.bank, self.before, self.loop = number % 2, number // 2, loop

    def full(self):
        return self.before + 1 + self.loop

    def earlier(self):
        return self.before + self.loop


FIRST = ["xT0", "xT1", "cT0", "q0", "cT1", "k", "q1", "V", "mT0"]
BODY = ["cT0", "cT1", "xT0", "xT1", "k", "q0", "mT1", "q1", "o0", "mT0", "V", "o1"]
LAST = ["eT", "mT1", "ef0", "ef1", "o0", "o1"]
SPLIT_FIRST = ["xT0", "xT1", "cT0", "q0", "cT1", "k", "q1"]
SPLIT = ["cT0", "cT1", "xT0", "xT1", "k", "q0", "q1"]


def fill_first(name):
    return Fill(FIRST.index(name))


def fill_body(name, i):
    return Fill(len(FIRST) + BODY.index(name), i * (len(BODY) // 2))


def fill_last(name):
    return Fill(len(FIRST) + len(BODY) * (PAIRS - 1) + LAST.index(name))


def flamingo_block(nc, x, ctx, g_attn, g_ffn, Wq, Wk, Wv, Wo, gate_w, up_w, down_w, fc1_w, fc2_w,
                   expert_w, gamma, beta, out):
    stack = ExitStack()
    with stack:
        def sb(name, shape, dt=FP32):
            return stack.enter_context(nc.sbuf_tensor(name, shape, dt))

        def sem(name):
            return stack.enter_context(nc.semaphore(name))

        store = sb("store", [P, 28736], FP32R)
        taken = [0]

        def part(cols, at=None):
            at = taken[0] if at is None else at
            taken[0] = max(taken[0], at + cols)
            return at

        def view(at, *dims):
            n = 1
            for d in dims:
                n *= d
            v = store[:, at:at + n]
            names = "abcde"[:len(dims)]
            if len(dims) > 1:
                v = v.rearrange(f"p ({' '.join(names)}) -> p {' '.join(names)}",
                                **{names[j]: dims[j] for j in range(1, len(dims))})
            return v

        a_wq, a_wk, a_wv = part(2 * KT * D), part(2 * KT * KVD), part(2 * KT * KVD)
        a_xT, a_cT, a_q = part(2 * KT * T), part(2 * KT * T), part(2 * KT * T)
        a_k = part(2 * T)
        part(2 * KT * T - 2 * T + 64)
        a_wo, a_oT = part(2 * KT * D), part(2 * KT * T)
        a_qs, a_ks = part(NPAIR * T), part(2 * KV * T)
        wq = view(a_wq, 2, KT, D)
        wk = view(a_wk, 2, KT, KVD)
        wv = view(a_wv, 2, KT, KVD)
        wo = view(a_wo, 2, KT, D)
        xT = view(a_xT, 2, KT, T)
        cT = view(a_cT, 2, KT, T)
        qT = view(a_q, 2, KT, T)
        kT = view(a_k, 2, T)
        oT = view(a_oT, 2, KT, T)
        qs = view(a_qs, 2, NPAIR, SEQ)
        ks = view(a_ks, 2, KV, 2, SEQ)

        up = view(0, 2, KT, INT)
        fc1 = view(8192, 2, KT, LAT)
        ef = view(10240, 2, LT, D)
        gw = view(12288, KT, 2, NE)
        x2T = view(12352, 2, KT, T)
        hT = view(a_wo, 2, MT, T)
        latT = view(a_oT, 2, LT, T)
        down = view(a_qs, 2, MT, D)

        xall = sb("xall", [P, NSEQ, D])
        ctxb = sb("ctxb", [P, 2, D])
        xn = sb("xn", [P, 2, D])
        probs = sb("probs", [P, 2, 4, 2, T])
        vpad = sb("vpad", [P, 2, KV, 3 * HD])
        onepad = sb("onepad", [P, 3 * HD])
        rden = sb("rden", [P, T])
        onorm = sb("onorm", [P, T])
        raw = sb("raw", [P, 5120])
        raw2 = sb("raw2", [P, 1568])
        raw_down = sb("raw_down", [P, DOWN_EARLY * D])
        expT = sb("expT", [P, LT, LAT])
        over = probs[:, :, :, :, :].rearrange("p u j e t -> p (u j e t)").rearrange("p (n b d) -> p n b d", n=4, b=2)
        relu, hfull, ysum = over[:, 0], over[:, 1], over[:, 2]
        scaled = over[:, 3]
        xg = sb("xg", [P, 2, D])
        gammab = sb("gammab", [P, D])
        betab = sb("betab", [P, D])
        logits = sb("logits", [P, 2, NE])
        top8 = sb("top8", [P, 2, 8])
        rw = sb("rw", [P, 2])
        mv2 = sb("mv2", [P, 2, 2])
        credit = sb("credit", [P, 18])
        st2 = sb("st2", [P, 2, 6])
        vare2 = sb("vare2", [P, 2])
        rstd2 = sb("rstd2", [P, 2])
        nbias2 = sb("nbias2", [P, 2])
        mx = sb("mx", [P, 2, NPAIR, 2])
        negmax = sb("negmax", [P, 2, MAXROWS, NPAIR])
        maxT = sb("maxT", [MAXROWS * NPAIR, 2, P], FP32R)
        ident = sb("ident", [P, P])
        maxsel = sb("maxsel", [P, 2])
        stats = sb("stats", [P, NSEQ, 6])
        mv = sb("mv", [P, NSEQ, 2])
        vare = sb("vare", [P, NSEQ])
        rstd = sb("rstd", [P, NSEQ])
        nbias = sb("nbias", [P, NSEQ])
        mhalf = sb("mhalf", [P, NSEQ])
        gates = sb("gates", [P, 2])
        tgates = sb("tgates", [P, 2])

        def bank(name):
            return stack.enter_context(nc.psum_tensor(name, [P, 512], FP32))

        s_bank = [bank("s_bank0"), bank("s_bank1")]
        st_bank = [bank("st_bank0"), bank("st_bank1")]
        o_bank = [bank("o_bank0"), bank("o_bank1")]
        g_bank = [bank("g_bank0"), bank("g_bank1")]

        x0_in, xrest_in, gates_in = sem("x0_in"), sem("xrest_in"), sem("gates_in")
        ctx_in = sem("ctx_in")
        wq_in, wkv_in, wo_in = sem("wq_in"), sem("wkv_in"), sem("wo_in")
        q_stacked = [sem("q_stacked0"), sem("q_stacked1")]
        k_stacked = [sem("k_stacked0"), sem("k_stacked1")]
        max_stacked = [sem("max_stacked0"), sem("max_stacked1")]
        stored = sem("stored")
        ident_zero, ident_ready, pool_const = sem("ident_zero"), sem("ident_ready"), sem("pool_const")
        ks_zero = sem("ks_zero")
        consts = sem("consts")
        wq_hi, wkv_hi, wo_hi = sem("wq_hi"), sem("wkv_hi"), sem("wo_hi")
        wq_lo, wkv_lo, wo_lo = sem("wq_lo"), sem("wkv_lo"), sem("wo_lo")
        var_ready, rstd_ready = sem("var_ready"), sem("rstd_ready")
        nbias_ready = sem("nbias_ready")
        xn_ready = sem("xn_ready")
        tanh_ready = sem("tanh_ready")
        g_full = [sem("g_full0"), sem("g_full1")]
        g_done = [sem("g_done0"), sem("g_done1")]
        g_hi = sem("g_hi")
        s_full, s_free = sem("s_full"), sem("s_free")
        st_full, st_free = sem("st_full"), sem("st_free")
        weighed, o_free = sem("weighed"), sem("o_free")
        rden_ready, oT_hi, oT_lo = sem("rden_ready"), sem("oT_hi"), sem("oT_lo")
        max_split = sem("max_split")
        up_in, small_in, down_in, affine_in = sem("up_in"), sem("small_in"), sem("down_in"), sem("affine_in")
        down_rest_in, fc1_lo = sem("down_rest_in"), sem("fc1_lo")
        up_hi, up_lo, down_hi, down_lo = sem("up_hi"), sem("up_lo"), sem("down_hi"), sem("down_lo")
        small_lo = sem("small_lo")
        affine_ready = sem("affine_ready")
        x2n_ready, x2_full, x2_hi, x2_lo = sem("x2n_ready"), sem("x2_full"), sem("x2_hi"), sem("x2_lo")
        up_full, up_free, h_full, h_hi, h_lo = sem("up_full"), sem("up_free"), sem("h_full"), sem("h_hi"), sem("h_lo")
        lat_full, lat_hi, lat_lo, logits_full, rw_ready = (
            sem("lat_full"), sem("lat_hi"), sem("lat_lo"), sem("logits_full"), sem("rw_ready"))
        down_full, y_ready, routed_full, routed_scaled = (
            sem("down_full"), sem("y_ready"), sem("routed_full"), sem("routed_scaled"))
        var2_ready, rstd2_ready, xg_ready, out_ready = (
            sem("var2_ready"), sem("rstd2_ready"), sem("xg_ready"), sem("out_ready"))
        own2 = sem("own2")
        waited = sem("waited")
        own = sem("own")

        def raw_view(t, at, n):
            return t[:, at:at + KT * n].rearrange("p (k n) -> p k n", k=KT)

        def x2_bank(i, b):
            bank = s_bank[b] if isinstance(i, int) and i == 0 else st_bank[b]
            return bank[:, :].rearrange("p (k t) -> p k t", k=KT)

        def wq_rows(a, k):
            return wq[:, a, k, :].rearrange("p (m r s) -> p m s r", m=KT, s=4)

        def wk_rows(a):
            return wk[:, a].rearrange("p k (d h) -> p k h d", h=KV)

        wk_raw = raw[:, 2048:2560].rearrange("p (k h d) -> p k h d", k=KT, h=KV)

        def down_raw(k):
            return raw_down[:, k * D:(k + 1) * D] if k < DOWN_EARLY else raw[:, (k - DOWN_EARLY) * D:(k - DOWN_EARLY + 1) * D]

        def wq_raw(k):
            return raw[:, k * D:(k + 1) * D].rearrange("p (s m r) -> p m s r", s=4, m=KT)

        def wait_apart(eng, signal, value):
            eng.wait_ge(signal, value)
            eng.sem_inc(waited, 1)

        block = stack.enter_context(nc.Block())

        @block.sync
        def _(sp):
            x_v = x.rearrange("s t d -> t s d")
            sp.dma_start(xall[:, 0:2, :], x_v[:, 0:2, :]).then_inc(x0_in, 16)
            sp.dma_start(raw[:, 0:2048].rearrange("p (k n) -> p k n", k=KT),
                         Wq.rearrange("(k p) n -> p k n", p=P)).then_inc(wq_in, 16)
            sp.dma_start(ctxb[:, :, :], ctx[0:2].rearrange("s t d -> t s d")).then_inc(ctx_in, 16)
            sp.dma_start(raw[:, 2048:2560].rearrange("p (k n) -> p k n", k=KT),
                         Wk.rearrange("(k p) n -> p k n", p=P)).then_inc(wkv_in, 16)
            sp.dma_start(raw[:, 2560:3072].rearrange("p (k n) -> p k n", k=KT),
                         Wv.rearrange("(k p) n -> p k n", p=P)).then_inc(wkv_in, 16)
            sp.dma_start(xall[:, 2:NSEQ, :], x_v[:, 2:NSEQ, :]).then_inc(xrest_in, 16)
            wo_v = Wo.rearrange("(hh j pp r) n -> hh pp j r n", hh=2, j=4, pp=2)
            for hh in range(2):
                for pp in range(2):
                    kt = 2 * hh + pp
                    sp.dma_start(raw[:, 3072 + kt * D:3072 + (kt + 1) * D], wo_v[hh, pp]).then_inc(wo_in, 16)
            sp.dma_start(gates[:, 0:1], g_attn.rearrange("(a b) -> a b", a=1).to_broadcast([P, 1])).then_inc(gates_in, 16)
            sp.dma_start(gates[:, 1:2], g_ffn.rearrange("(a b) -> a b", a=1).to_broadcast([P, 1])).then_inc(gates_in, 16)

            def load_ctx(i, F):
                f = F("cT1")
                wait_apart(sp, g_full[f.bank], f.full())
                sp.dma_start(ctxb[:, :, :], ctx[bass.ds(2 * i, 2)].rearrange("s t d -> t s d")).then_inc(ctx_in, 16)

            def hi_ready(name, a):
                order = SPLIT_FIRST if isinstance(a, int) and a == 0 else SPLIT
                wait_apart(sp, g_hi, len(SPLIT) * a + order.index(name) + 1)

            def all_ready(name, F):
                f = F(name)
                wait_apart(sp, g_done[f.bank], f.full())

            def stack_k(b, F, a, st_done):
                hi_ready("k", a)
                if st_done is not None:
                    wait_apart(sp, st_full, st_done)
                for term, src in ((0, 0), (2, 0), (1, 1)):
                    if src == 1: all_ready("k", F)
                    for par in range(2):
                        at = (2 * term + par) * HD
                        sp.dma_start(ks[at:at + HD, b, :, par, :].bitcast(FP32),
                                     kT[:, src, b * SEQ:(b + 1) * SEQ].bitcast(FP32)).then_inc(k_stacked[b], 16)

            def stack_q(b, F, a):
                all_ready("q0", F)
                hi_ready("q1", a)
                for term, src in enumerate((0, 0, 1)):
                    if src == 1: all_ready("q1", F)
                    sp.dma_start(qs[2 * HD * term:2 * HD * (term + 1), b, :, :].bitcast(FP32),
                                 qT[:, src, :, b * SEQ:(b + 1) * SEQ].bitcast(FP32)).then_inc(q_stacked[b], 16)

            load_ctx(1, fill_first)
            sp.wait_ge(ks_zero, 1)
            stack_k(0, fill_first, 0, None)
            stack_q(0, fill_first, 0)
            stack_k(1, fill_first, 0, None)
            stack_q(1, fill_first, 0)

            sp.wait_ge(max_stacked[0], 16)
            sp.wait_ge(wq_lo, KT)
            sp.wait_ge(wkv_lo, 2)
            sp.wait_ge(wo_lo, 1)
            sp.dma_start(raw[:, 0:KT * INT].rearrange("p (k n) -> p k n", k=KT),
                         up_w.rearrange("(k p) n -> p k n", p=P)).then_inc(up_in, 16)
            sp.dma_start(raw[:, KT * INT:KT * (INT + LAT)].rearrange("p (k n) -> p k n", k=KT),
                         fc1_w.rearrange("(k p) n -> p k n", p=P)).then_inc(up_in, 16)
            sp.dma_start(raw2[:, 0:512].rearrange("p (k n) -> p k n", k=LT),
                         expert_w.rearrange("(k p) n -> p k n", p=P)).then_inc(small_in, 16)
            sp.dma_start(raw2[:, 512:1536].rearrange("p (k n) -> p k n", k=LT),
                         fc2_w.rearrange("(k p) n -> p k n", p=P)).then_inc(small_in, 16)
            sp.dma_start(raw2[:, 1536:1568].rearrange("p (k n) -> p k n", k=KT),
                         gate_w.rearrange("(k p) n -> p k n", p=P)).then_inc(small_in, 16)
            sp.dma_start(gammab[:, :], gamma.rearrange("(a b) -> a b", a=1).to_broadcast([P, D])).then_inc(affine_in, 16)
            sp.dma_start(betab[:, :], beta.rearrange("(a b) -> a b", a=1).to_broadcast([P, D])).then_inc(affine_in, 16)

            down_v = down_w.rearrange("(k p) n -> p k n", p=P)
            sp.dma_start(raw_down[:, :].rearrange("p (k n) -> p k n", k=DOWN_EARLY),
                         down_v[:, 0:DOWN_EARLY, :]).then_inc(down_in, 16)

            def body(i, more):
                def F(name):
                    return fill_body(name, i)
                stack_k(0, F, i + 1, 16 * i + 8)
                stack_q(0, F, i + 1)
                if more: load_ctx(i + 2, F)
                stack_k(1, F, i + 1, 16 * i + 16)
                stack_q(1, F, i + 1)

            with sp.Fori(0, PAIRS - 2) as i:
                body(i, True)
            body(PAIRS - 2, False)
            sp.wait_ge(up_lo, 2)
            sp.dma_start(raw[:, 0:(MT - DOWN_EARLY) * D].rearrange("p (k n) -> p k n", k=MT - DOWN_EARLY),
                         down_v[:, DOWN_EARLY:MT, :]).then_inc(down_rest_in, 16)
            with sp.Fori(0, PAIRS - 1) as i:
                wait_apart(sp, out_ready, 2 * i + 2 + 2)
                sp.dma_start(out[bass.ds(2 * i, 2)].rearrange("s t d -> t s d"),
                             xall[:, bass.ds(2 * i, 2), :]).then_inc(stored, 16)
            for n in range(NSEQ - 2, NSEQ):
                sp.wait_ge(out_ready, n + 1 + 2)
                sp.dma_start(out[n], xall[:, n, :]).then_inc(stored, 16)
            sp.wait_ge(stored, 16 * (PAIRS + 1))

        @block.gpsimd
        def _(pool):
            nc.gpsimd.memset(ident[:, :], 0.0).then_inc(ident_zero, 1)
            pool.wait_ge(ident_zero, 1)
            nc.gpsimd.affine_select(out=ident[:, :], in_=ident[:, :], compare_op=ALU.not_equal, fill=1.0,
                                    base=0, pattern=[[-1, P]], channel_multiplier=1).then_inc(ident_ready, 1)
            nc.gpsimd.memset(mhalf[:, :], -0.5).then_inc(pool_const, 1)
            nc.gpsimd.memset(ks[0:STACK, :, :, :, :].rearrange("p s h e t -> p (s h e t)").bitcast(FP32),
                             0.0).then_inc(ks_zero, 1)
            nc.gpsimd.memset(onepad[:, :], 0.0).then_inc(pool_const, 1)
            pool.wait_ge(pool_const, 2)
            nc.gpsimd.memset(onepad[:, HD:2 * HD], 1.0).then_inc(pool_const, 1)
            nc.gpsimd.memset(vpad[:, :, :, :], 0.0).then_inc(pool_const, 1)
            pool.wait_ge(var_ready, 1)
            nc.gpsimd.tensor_tensor(rstd[:, 0:2], vare[:, 0:2], mhalf[:, 0:2], ALU.pow).then_inc(rstd_ready, 1)
            for k in (2, 3):
                pool.wait_ge(wq_hi, k)
                nc.gpsimd.tensor_tensor(wq_rows(1, k), wq_raw(k), wq_rows(0, k).bitcast(FP32), ALU.subtract).then_inc(wq_lo, 1)
            pool.wait_ge(var_ready, 2)
            nc.gpsimd.tensor_tensor(rstd[:, 2:NSEQ], vare[:, 2:NSEQ], mhalf[:, 2:NSEQ], ALU.pow).then_inc(rstd_ready, 1)
            pool.wait_ge(wo_in, 64)
            pool.wait_ge(wo_hi, 1)
            nc.gpsimd.tensor_tensor(wo[:, 1], raw_view(raw, 3072, D), wo[:, 0].bitcast(FP32),
                                    ALU.subtract).then_inc(wo_lo, 1)
            pool.wait_ge(affine_in, 32)
            pool.wait_ge(tanh_ready, 1)
            for t in (gammab, betab):
                nc.gpsimd.tensor_scalar(t[:, :], t[:, :], tgates[:, 1:2], None, ALU.mult).then_inc(affine_ready, 1)
            def inverse_std(value, lo=0, hi=2):
                pool.wait_ge(var2_ready, value)
                nc.gpsimd.tensor_tensor(rstd2[:, lo:hi], vare2[:, lo:hi], mhalf[:, lo:hi], ALU.pow).then_inc(rstd2_ready, 1)

            def body(i, more):
                pool.wait_ge(affine_ready, 2)
                for b in range(2):
                    pool.wait_ge(out_ready, 2 * i + b + 1)
                    nc.gpsimd.tensor_tensor(xg[:, b:b + 1, :], xall[:, bass.ds(2 * i + b, 1), :],
                                            betab[:, :].unsqueeze(1), ALU.add).then_inc(xg_ready, 1)
                if more:
                    inverse_std(2 * i + 2)
                    inverse_std(2 * i + 3)
                else:
                    for b in range(2):
                        inverse_std(2 * i + 2 + b, b, b + 1)

            for k in range(KT):
                if k == 1: inverse_std(1)
                pool.wait_ge(up_hi, k + 1)
                nc.gpsimd.tensor_tensor(up[:, 1, k, :], raw[:, k * INT:(k + 1) * INT],
                                        up[:, 0, k, :].bitcast(FP32), ALU.subtract).then_inc(up_lo, 1)
            for k in range(MT // 2, MT):
                pool.wait_ge(down_hi, k + 1)
                nc.gpsimd.tensor_tensor(down[:, 1, k, :], down_raw(k), down[:, 0, k, :].bitcast(FP32),
                                        ALU.subtract).then_inc(down_lo, 1)

            f = fill_last("o1")
            pool.wait_ge(g_done[f.bank], f.full())
            with pool.Fori(0, PAIRS - 1) as i:
                body(i, True)
            body(PAIRS - 1, False)

        @block.scalar
        def _(act):
            def take_hi(name, F, dst, src_cols=512):
                f = F(name)
                act.wait_ge(g_full[f.bank], f.full())
                nc.scalar.activation(dst, g_bank[f.bank][:, 0:src_cols] if len(dst.shape) == 2 else
                                     g_bank[f.bank][:, 0:src_cols].rearrange("p (k t) -> p k t", k=dst.shape[1]),
                                     ACT.Copy).then_inc(g_hi, 1)

            def hi_of(name, F):
                if name[:2] in ("xT", "cT"):
                    b = int(name[2])
                    take_hi(name, F, (xT if name[0] == "x" else cT)[:, 0, :, b * SEQ:(b + 1) * SEQ])
                elif name[0] == "q":
                    m = 2 * int(name[1])
                    take_hi(name, F, qT[:, 0, m:m + 2, :])
                elif name == "k":
                    take_hi(name, F, kT[:, 0, :], T)

            act.wait_ge(wq_in, 16)
            for k in (0, 2, 3):
                nc.scalar.activation(wq_rows(0, k), wq_raw(k), ACT.Copy).then_inc(wq_hi, 1)
            hi_of("xT0", fill_first)
            hi_of("xT1", fill_first)
            act.wait_ge(wkv_in, 32)
            nc.scalar.activation(wk_rows(0), wk_raw, ACT.Copy).then_inc(wkv_hi, 1)
            nc.scalar.activation(wv[:, 0], raw_view(raw, 2560, KVD), ACT.Copy).then_inc(wkv_hi, 1)

            def take_v(F):
                f = F("V")
                act.wait_ge(g_full[f.bank], f.full())
                nc.scalar.activation(vpad[:, :, :, HD:2 * HD],
                                     g_bank[f.bank][:, 0:T].rearrange("p (s h d) -> p s h d", s=2, h=KV),
                                     ACT.Copy).then_inc(g_done[f.bank], 1)

            def take_max(b, F):
                f = F(f"mT{b}")
                act.wait_ge(g_full[f.bank], f.full())
                nc.scalar.activation(maxT[:, b, :], g_bank[f.bank][0:MAXROWS * NPAIR, 0:P],
                                     ACT.Copy).then_inc(g_done[f.bank], 1)
                wait_apart(act, g_done[f.bank], f.full())
                act.dma_start(qs[STACK:STACK + MAXROWS, b, :, :].bitcast(FP32),
                              maxT[:, b, :].bitcast(FP32)).then_inc(max_stacked[b], 16)

            def normalize(i):
                for b in range(2):
                    nc.scalar.activation(xn[:, b:b + 1, :], xall[:, bass.ds(2 * i + b, 1), :], ACT.Identity,
                                         bias=nbias[:, bass.ds(2 * i + b, 1)],
                                         scale=rstd[:, bass.ds(2 * i + b, 1)]).then_inc(xn_ready, 1)

            def exp_step(i, t):
                act.wait_ge(st_full, 16 * i + t + 1)
                g = t // 4
                if t % 4 == 0:
                    act.wait_ge(weighed, 4 * i + g + 1)
                nc.scalar.activation(probs[:, g % 2, t % 4, :, :],
                                     st_bank[t % 2][:, :].rearrange("p (a b) -> p a b", a=2),
                                     ACT.Exp, scale=SCALE).then_inc(st_free, 1)

            for name in SPLIT_FIRST[2:]:
                hi_of(name, fill_first)
            act.wait_ge(wo_in, 64)
            nc.scalar.activation(wo[:, 0], raw_view(raw, 3072, D), ACT.Copy).then_inc(wo_hi, 1)
            act.wait_ge(gates_in, 32)
            nc.scalar.activation(tgates[:, :], gates[:, :], ACT.Tanh).then_inc(tanh_ready, 1)
            act.wait_ge(pool_const, 4)
            take_v(fill_first)
            take_max(0, fill_first)
            for t in range(4):
                exp_step(0, t)
            act.wait_ge(nbias_ready, 1)
            with act.Fori(0, PAIRS - 1) as i:
                def F(name):
                    return fill_body(name, i)
                normalize(i + 1)
                for t in range(4, 8):
                    exp_step(i, t)
                    hi_of(("cT0", "cT1", "xT0", "xT1")[t - 4], F)
                for b in range(2):
                    act.wait_ge(k_stacked[b], 96 * (i + 1))
                    act.wait_ge(q_stacked[b], 48 * (i + 1))
                hi_of("k", F)
                hi_of("q0", F)
                take_max(1, F)
                exp_step(i, 8)
                exp_step(i, 9)
                hi_of("q1", F)
                for t in range(10, 16):
                    exp_step(i, t)
                take_max(0, F)
                take_v(F)
                for t in range(4):
                    exp_step(i + 1, t)
            for t in range(4, 8):
                exp_step(PAIRS - 1, t)
            f = fill_last("eT")
            act.wait_ge(g_full[f.bank], f.full())
            nc.scalar.activation(expT[:, :, :], g_bank[f.bank][:, :].rearrange("p (k n) -> p k n", k=LT),
                                 ACT.Copy).then_inc(g_done[f.bank], 1)
            f = fill_body("V", PAIRS - 2)
            act.wait_ge(g_full[f.bank], f.full())
            for b in range(2):
                act.wait_ge(k_stacked[b], 96 * PAIRS)
                act.wait_ge(q_stacked[b], 48 * PAIRS)
            act.wait_ge(up_in, 32)
            act.wait_ge(small_in, 48)

            def up_hi_part(k):
                nc.scalar.activation(up[:, 0, k, :], raw[:, k * INT:(k + 1) * INT], ACT.Copy).then_inc(up_hi, 1)

            up_hi_part(0)
            take_max(1, fill_last)
            for k in range(1, KT):
                up_hi_part(k)

            def ef_hi_part(l):
                f = fill_last(f"ef{l}")
                act.wait_ge(g_full[f.bank], f.full())
                nc.scalar.activation(ef[:, 0, l, :], g_bank[f.bank][:, :], ACT.Copy).then_inc(g_hi, 1)

            def x2_hi_part(i, b):
                act.wait_ge(x2_full, 2 * i + b + 1)
                nc.scalar.activation(x2T[:, 0, :, b * SEQ:(b + 1) * SEQ], x2_bank(i, b), ACT.Copy).then_inc(x2_hi, 1)

            ef_hi_part(0)
            exp_step(PAIRS - 1, 8)
            exp_step(PAIRS - 1, 9)
            x2_hi_part(0, 0)
            x2_hi_part(0, 1)
            exp_step(PAIRS - 1, 10)
            exp_step(PAIRS - 1, 11)
            ef_hi_part(1)
            for t in range(12, 16):
                exp_step(PAIRS - 1, t)
            nc.scalar.activation(fc1[:, 0], raw_view(raw, KT * INT, LAT), ACT.Copy)
            nc.scalar.activation(gw[:, :, 0, :], raw_view(raw2, 1536, NE), ACT.Copy).then_inc(up_hi, 1)

            act.wait_ge(down_in, 16)
            act.wait_ge(st_full, 16 * PAIRS)
            for k in range(MT):
                if k == DOWN_EARLY: act.wait_ge(down_rest_in, 16)
                nc.scalar.activation(down[:, 0, k, :], down_raw(k), ACT.Copy).then_inc(down_hi, 1)

            def ffn(i, more):
                for u in range(MT // 2):
                    act.wait_ge(up_full, 4 * i + u + 1)
                    nc.scalar.activation(relu[:, u % 2, :], s_bank[u % 2][:, :], ACT.Relu).then_inc(up_free, 1)
                    act.wait_ge(up_free, 4 * i + u + 1 + 2)
                    act.wait_ge(h_lo, 4 * i + u + 1)
                    nc.scalar.activation(hfull[:, u % 2, :], relu[:, u % 2, :], ACT.Square).then_inc(h_full, 1)
                act.wait_ge(lat_full, i + 1)
                nc.scalar.activation(latT[:, 0], o_bank[0][:, :].rearrange("p (k t) -> p k t", k=LT),
                                     ACT.Copy).then_inc(lat_hi, 1)
                if more:
                    for b in range(2):
                        x2_hi_part(i + 1, b)
                for b in range(2):
                    act.wait_ge(routed_full, 2 * i + b + 1)
                    act.wait_ge(rw_ready, i + 1)
                    act.wait_ge(y_ready, 2 * i + b + 1)
                    nc.scalar.activation(scaled[:, b, :], o_bank[b][:, :], ACT.Copy,
                                         scale=rw[:, b:b + 1]).then_inc(routed_scaled, 1)

            with act.Fori(0, PAIRS - 1) as i:
                ffn(i, True)
            ffn(PAIRS - 1, False)

        @block.vector
        def _(dve):
            count = [0]

            def mine(ins):
                count[0] += 1
                ins.then_inc(own, 1)
                dve.wait_ge(own, count[0])

            for n, free in enumerate((s_free, st_free, o_free, weighed, up_free, h_lo, y_ready, routed_scaled, out_ready)):
                for m in range(2):
                    nc.vector.memset(credit[:, 2 * n + m:2 * n + m + 1], 0.0).then_inc(free, 1)

            def ln_stats(lo, hi):
                for s in range(lo, hi):
                    last = nc.vector.bn_stats(stats[:, s, :], xall[:, s, :])
                mine(last)
                for s in range(lo, hi):
                    last = nc.vector.bn_aggr(mv[:, s, :], stats[:, s, :])
                mine(last)
                nc.vector.tensor_scalar(vare[:, lo:hi], mv[:, lo:hi, 1], EPS, None, ALU.add).then_inc(var_ready, 1)

            def ln_bias(lo, hi, which):
                dve.wait_ge(rstd_ready, which)
                mine(nc.vector.scalar_tensor_tensor(out=nbias[:, lo:hi], in0=mv[:, lo:hi, 0], scalar=-1.0,
                                                    in1=rstd[:, lo:hi], op0=ALU.mult, op1=ALU.mult))

            def normalize(i):
                for b in range(2):
                    nc.vector.tensor_scalar(xn[:, b:b + 1, :], xall[:, bass.ds(2 * i + b, 1), :],
                                            rstd_col(rstd, i, b), rstd_col(nbias, i, b),
                                            ALU.mult, ALU.add).then_inc(xn_ready, 1)

            def rstd_col(t, i, b):
                return t[:, bass.ds(2 * i + b, 1)]

            def take_lo(name, F, a):
                f = F(name)
                order = SPLIT_FIRST if F is fill_first else SPLIT
                dve.wait_ge(g_hi, len(SPLIT) * a + order.index(name) + 1)
                if name[:2] in ("xT", "cT"):
                    b = int(name[2])
                    t = xT if name[0] == "x" else cT
                    dst, hi = t[:, 1, :, b * SEQ:(b + 1) * SEQ], t[:, 0, :, b * SEQ:(b + 1) * SEQ]
                    src = g_bank[f.bank][:, :].rearrange("p (k t) -> p k t", k=KT)
                elif name[0] == "q":
                    m = 2 * int(name[1])
                    dst, hi = qT[:, 1, m:m + 2, :], qT[:, 0, m:m + 2, :]
                    src = g_bank[f.bank][:, :].rearrange("p (k t) -> p k t", k=2)
                else:
                    dst, hi, src = kT[:, 1, :], kT[:, 0, :], g_bank[f.bank][:, 0:T]
                nc.vector.tensor_tensor(dst, src, hi.bitcast(FP32), ALU.subtract).then_inc(g_done[f.bank], 1)

            def row_max(i, s):
                dve.wait_ge(s_full, 16 * i + s + 1)
                b, h = s // 8, s % 8
                nc.vector.reduce_max(mx[:, b, 2 * h:2 * h + 2, :],
                                     s_bank[s % 2][:, :].rearrange("p (a e k) -> p a e k", a=2, e=2),
                                     AX.X).then_inc(s_free, 1)

            def split_max(i, b):
                dve.wait_ge(s_free, 16 * i + 8 * b + 8 + 2)
                v = negmax[:, b].rearrange("p (e l) n -> p e l n", e=2)
                m = mx[:, b].rearrange("p n e -> p e n")
                nc.vector.tensor_scalar(v[:, :, 0, :].bitcast(FP32R), m, -1.0, None, ALU.mult).then_inc(max_split, 1)
                dve.wait_ge(max_split, 4 * i + 2 * b + 1)
                nc.vector.scalar_tensor_tensor(out=v[:, :, 1, :].bitcast(FP32R), in0=m, scalar=-1.0,
                                               in1=v[:, :, 0, :], op0=ALU.mult, op1=ALU.subtract).then_inc(max_split, 1)

            def head_outputs(i, g):
                b, hh = g // 2, g % 2
                bank = o_bank[g % 2]
                dve.wait_ge(weighed, 4 * i + g + 1 + 2)
                nc.vector.reciprocal(rden[:, :], bank[:, T:2 * T]).then_inc(rden_ready, 1)
                dve.wait_ge(rden_ready, 4 * i + g + 1)
                nc.vector.tensor_tensor(onorm[:, :], bank[:, 0:T], rden[:, :], ALU.mult).then_inc(o_free, 1)
                dve.wait_ge(o_free, 4 * i + g + 1 + 2)
                on = onorm[:, :].rearrange("p (k t) -> p k t", k=2)
                hi = oT[:, 0, 2 * hh:2 * hh + 2, b * SEQ:(b + 1) * SEQ]
                nc.vector.tensor_copy(hi, on).then_inc(oT_hi, 1)
                dve.wait_ge(oT_hi, 4 * i + g + 1)
                nc.vector.tensor_tensor(oT[:, 1, 2 * hh:2 * hh + 2, b * SEQ:(b + 1) * SEQ], on,
                                        hi.bitcast(FP32), ALU.subtract).then_inc(oT_lo, 1)

            def add_attention(i, b, F):
                f = F(f"o{b}")
                dve.wait_ge(g_full[f.bank], f.full())
                xb = xall[:, bass.ds(2 * i + b, 1), :].rearrange("p a d -> p (a d)")
                nc.vector.scalar_tensor_tensor(out=xb, in0=g_bank[f.bank][:, :], scalar=tgates[:, 0:1], in1=xb,
                                               op0=ALU.mult, op1=ALU.add).then_inc(g_done[f.bank], 1)

            dve.wait_ge(ident_ready, 1)
            for par in range(2):
                last = nc.vector.reduce_sum(maxsel[:, par:par + 1],
                                            ident[:, STACK + 2 * par:STACK + 2 * par + 2], AX.X)
            mine(last)
            for par in range(2):
                last = nc.vector.tensor_scalar(
                    ks[STACK:P, :, :, par, :].rearrange("p s h t -> p (s h) t"),
                    ident[STACK:P, 0:1].unsqueeze(2).to_broadcast([32, 2 * KV, SEQ]), 0.0,
                    maxsel[STACK:P, par:par + 1], ALU.mult, ALU.add)
            last.then_inc(consts, 1)
            dve.wait_ge(x0_in, 16)
            ln_stats(0, 2)
            ln_bias(0, 2, 1)
            normalize(0)
            dve.wait_ge(wq_in, 16)
            mine(nc.vector.tensor_copy(wq_rows(0, 1), wq_raw(1)))
            dve.wait_ge(wq_hi, 1)
            for k in (1, 0):
                nc.vector.tensor_tensor(wq_rows(1, k), wq_raw(k), wq_rows(0, k).bitcast(FP32), ALU.subtract).then_inc(wq_lo, 1)
            take_lo("xT0", fill_first, 0)
            take_lo("xT1", fill_first, 0)
            dve.wait_ge(wkv_hi, 2)
            nc.vector.tensor_tensor(wk_rows(1), wk_raw, wk_rows(0).bitcast(FP32), ALU.subtract).then_inc(wkv_lo, 1)
            nc.vector.tensor_tensor(wv[:, 1], raw_view(raw, 2560, KVD), wv[:, 0].bitcast(FP32), ALU.subtract).then_inc(wkv_lo, 1)
            for name in SPLIT_FIRST[2:]:
                take_lo(name, fill_first, 0)
            dve.wait_ge(xrest_in, 16)
            ln_stats(2, NSEQ)
            for s in range(8):
                row_max(0, s)
            split_max(0, 0)
            ln_bias(2, NSEQ, 2)
            nc.vector.memset(credit[:, 0:1], 0.0).then_inc(nbias_ready, 1)
            dve.wait_ge(tanh_ready, 1)
            for s in range(8, 12):
                row_max(0, s)
            with dve.Fori(0, PAIRS - 1) as i:
                def F(name):
                    return fill_body(name, i)
                for s in range(12, 16):
                    row_max(i, s)
                    take_lo(("cT0", "cT1", "xT0", "xT1")[s - 12], F, i + 1)
                split_max(i, 1)
                take_lo("k", F, i + 1)
                head_outputs(i, 0)
                take_lo("q0", F, i + 1)
                head_outputs(i, 1)
                take_lo("q1", F, i + 1)
                add_attention(i, 0, F)
                for s in range(8):
                    row_max(i + 1, s)
                split_max(i + 1, 0)
                head_outputs(i, 2)
                head_outputs(i, 3)
                row_max(i + 1, 8)
                row_max(i + 1, 9)
                row_max(i + 1, 10)
                row_max(i + 1, 11)
                add_attention(i, 1, F)

            seen = [0]

            def chained(ins, i):
                seen[0] += 1
                ins.then_inc(own2, 1)
                wait_apart(dve, own2, OWN2 * i + seen[0])

            def inverse_std(src, i, which, seqs=(0, 1)):
                for b in seqs:
                    last = nc.vector.bn_stats(st2[:, b, :], src(b))
                chained(last, i)
                for b in seqs:
                    last = nc.vector.bn_aggr(mv2[:, b, :], st2[:, b, :])
                chained(last, i)
                lo, hi = seqs[0], seqs[-1] + 1
                nc.vector.tensor_scalar(vare2[:, lo:hi], mv2[:, lo:hi, 1], EPS, None, ALU.add).then_inc(var2_ready, 1)
                dve.wait_ge(rstd2_ready, which)

            def normalize2(i, which, a):
                inverse_std(lambda b: xall[:, bass.ds(2 * a + b, 1), :].rearrange("p a d -> p (a d)"), i, which)
                chained(nc.vector.scalar_tensor_tensor(out=nbias2[:, :], in0=mv2[:, :, 0], scalar=-1.0,
                                                       in1=rstd2[:, :], op0=ALU.mult, op1=ALU.mult), i)
                for b in range(2):
                    nc.vector.tensor_scalar(xn[:, b:b + 1, :], xall[:, bass.ds(2 * a + b, 1), :],
                                            rstd2[:, b:b + 1], nbias2[:, b:b + 1],
                                            ALU.mult, ALU.add).then_inc(x2n_ready, 1)

            def x2_lo_part(i, b):
                dve.wait_ge(x2_hi, 2 * i + b + 1)
                nc.vector.tensor_tensor(x2T[:, 1, :, b * SEQ:(b + 1) * SEQ], x2_bank(i, b),
                                        x2T[:, 0, :, b * SEQ:(b + 1) * SEQ].bitcast(FP32),
                                        ALU.subtract).then_inc(x2_lo, 1)

            for s in range(12, 16):
                row_max(PAIRS - 1, s)
            split_max(PAIRS - 1, 1)
            normalize2(0, 1, 0)
            head_outputs(PAIRS - 1, 0)
            head_outputs(PAIRS - 1, 1)

            def ef_lo_part(l):
                f = fill_last(f"ef{l}")
                dve.wait_ge(g_hi, len(SPLIT) * PAIRS + l + 1)
                nc.vector.tensor_tensor(ef[:, 1, l, :], g_bank[f.bank][:, :], ef[:, 0, l, :].bitcast(FP32),
                                        ALU.subtract).then_inc(g_done[f.bank], 1)

            ef_lo_part(0)
            ef_lo_part(1)
            head_outputs(PAIRS - 1, 2)
            head_outputs(PAIRS - 1, 3)
            for b in range(2):
                x2_lo_part(0, b)
            dve.wait_ge(up_hi, 5)
            nc.vector.tensor_tensor(gw[:, :, 1, :], raw_view(raw2, 1536, NE), gw[:, :, 0, :].bitcast(FP32),
                                    ALU.subtract).then_inc(small_lo, 1)
            nc.vector.tensor_tensor(fc1[:, 1], raw_view(raw, KT * INT, LAT), fc1[:, 0].bitcast(FP32),
                                    ALU.subtract).then_inc(fc1_lo, 1)
            for k in range(MT // 2):
                dve.wait_ge(down_hi, k + 1)
                nc.vector.tensor_tensor(down[:, 1, k, :], down_raw(k), down[:, 0, k, :].bitcast(FP32),
                                        ALU.subtract).then_inc(down_lo, 1)
            for b in range(2):
                add_attention(PAIRS - 1, b, fill_last)

            start2 = seen[0]

            def ffn(i, more):
                seen[0] = start2
                if more:
                    normalize2(i, 2 * i + 2, i + 1)
                for u in range(MT // 2):
                    dve.wait_ge(h_full, 4 * i + u + 1)
                    src = hfull[:, u % 2, :].rearrange("p (m t) -> p m t", m=2)
                    nc.vector.tensor_copy(hT[:, 0, 2 * u:2 * u + 2, :], src).then_inc(h_hi, 1)
                    dve.wait_ge(h_hi, 4 * i + u + 1)
                    nc.vector.tensor_tensor(hT[:, 1, 2 * u:2 * u + 2, :], src,
                                            hT[:, 0, 2 * u:2 * u + 2, :].bitcast(FP32), ALU.subtract).then_inc(h_lo, 1)
                dve.wait_ge(lat_hi, i + 1)
                nc.vector.tensor_tensor(latT[:, 1], o_bank[0][:, :].rearrange("p (k t) -> p k t", k=LT),
                                        latT[:, 0].bitcast(FP32), ALU.subtract).then_inc(lat_lo, 1)
                wait_apart(dve, logits_full, i + 1)
                both = o_bank[1][:, 0:4 * NE].rearrange("p (b h e) -> p b h e", b=2, h=2)
                chained(nc.vector.tensor_copy(logits[:, :, :], both[:, :, 1, :]), i)
                chained(nc.vector.tensor_tensor(logits[:, :, :], both[:, :, 0, :], logits[:, :, :], ALU.add), i)
                for b in range(2):
                    last = nc.vector.max(top8[:, b, :], logits[:, b, :])
                chained(last, i)
                nc.vector.tensor_tensor(rw[:, :], top8[:, :, 0], top8[:, :, 1], ALU.add).then_inc(rw_ready, 1)
                if more:
                    for b in range(2):
                        x2_lo_part(i + 1, b)
                def add_branches(b):
                    dve.wait_ge(down_full, 2 * i + b + 1)
                    dve.wait_ge(routed_scaled, 2 * i + b + 1 + 2)
                    nc.vector.tensor_tensor(ysum[:, b, :], g_bank[b][:, :], scaled[:, b, :], ALU.add).then_inc(y_ready, 1)

                def layer_norm(seqs, which):
                    inverse_std(lambda b: ysum[:, b, :], i, which, seqs)
                    dve.wait_ge(affine_ready, 2)
                    for b in seqs:
                        last = nc.vector.scalar_tensor_tensor(out=ysum[:, b, :], in0=ysum[:, b, :], scalar=mv2[:, b, 0:1],
                                                              in1=gammab[:, :], op0=ALU.subtract, op1=ALU.mult)
                    chained(last, i)
                    dve.wait_ge(xg_ready, 2 * i + 2)
                    for b in seqs:
                        nc.vector.scalar_tensor_tensor(out=xall[:, bass.ds(2 * i + b, 1), :].rearrange("p a d -> p (a d)"),
                                                       in0=ysum[:, b, :], scalar=rstd2[:, b:b + 1], in1=xg[:, b, :],
                                                       op0=ALU.mult, op1=ALU.add).then_inc(out_ready, 1)

                if more:
                    for b in range(2):
                        add_branches(b)
                    dve.wait_ge(y_ready, 2 * i + 2 + 2)
                    layer_norm((0, 1), 2 * i + 3)
                else:
                    for b in range(2):
                        add_branches(b)
                        dve.wait_ge(y_ready, 2 * i + b + 1 + 2)
                        layer_norm((b,), 2 * i + 2 + b)

            with dve.Fori(0, PAIRS - 1) as i:
                ffn(i, True)
                assert seen[0] == start2 + OWN2
            ffn(PAIRS - 1, False)

        @block.tensor
        def _(pe):
            def keep_warm(n, bank=o_bank[0]):
                for _ in range(n):
                    nc.tensor.matmul(bank[:, 0:P], ident[:, :], ident[:, :], start=True, stop=True)

            def claim(name, F):
                f = F(name)
                if not (isinstance(f.earlier(), int) and f.earlier() == 0):
                    pe.wait_ge(g_done[f.bank], f.earlier())
                return f

            def ready(name, F):
                f = F(name)
                pe.wait_ge(g_done[f.bank], f.full())

            def transposed(name, F, src):
                f = claim(name, F)
                for k in range(KT):
                    last = nc.tensor.transpose(g_bank[f.bank][:, k * P:(k + 1) * P], src[:, k * P:(k + 1) * P],
                                               ident[:, :])
                last.then_inc(g_full[f.bank], 1)

            def three(dst, lhs, rhs, tiles):
                n = 0
                for k in range(tiles):
                    for a, c in ((0, 0), (0, 1), (1, 0)):
                        last = nc.tensor.matmul(dst, lhs(a, k), rhs(c, k), start=(n == 0), stop=(n == 3 * tiles - 1))
                        n += 1
                return last

            def project_q_tile(m, F):
                f = F(f"q{m // 2}")
                last = three(g_bank[f.bank][:, m % 2 * T:(m % 2 + 1) * T], lambda a, k: wq[:, a, k, m * P:(m + 1) * P],
                             lambda c, k: xT[:, c, k, :], KT)
                if m % 2: last.then_inc(g_full[f.bank], 1)

            def project_k(F):
                f = claim("k", F)
                three(g_bank[f.bank][:, 0:T], lambda a, k: wk[:, a, k, :], lambda c, k: cT[:, c, k, :],
                      KT).then_inc(g_full[f.bank], 1)

            def project_v(F):
                f = claim("V", F)
                for b in range(2):
                    last = three(g_bank[f.bank][:, b * KVD:(b + 1) * KVD],
                                 lambda a, k: cT[:, a, k, b * SEQ:(b + 1) * SEQ], lambda c, k: wv[:, c, k, :], KT)
                last.then_inc(g_full[f.bank], 1)

            def scores(i, s):
                b, h = s // 8, s % 8
                if h == 0:
                    pe.wait_ge(k_stacked[b], 96 * (i + 1))
                    pe.wait_ge(q_stacked[b], 48 * (i + 1))
                pe.wait_ge(s_free, 16 * i + s + 1)
                for p in range(2):
                    last = nc.tensor.matmul(s_bank[s % 2][:, p * T:(p + 1) * T], qs[0:STACK, b, 2 * h + p, :],
                                            ks[0:STACK, b, h, :, :], start=True, stop=True)
                last.then_inc(s_full, 1)

            def transpose_max(i, b, F):
                f = claim(f"mT{b}", F)
                wait_apart(pe, max_split, 4 * i + 2 * b + 2)
                nc.tensor.transpose(g_bank[f.bank][0:MAXROWS * NPAIR, 0:P],
                                    negmax[:, b].rearrange("p r n -> p (r n)"), ident[:, :]).then_inc(g_full[f.bank], 1)

            def scores_t(i, t):
                b, h = t // 8, t % 8
                if h == 0:
                    pe.wait_ge(max_stacked[b], 16 * (i + 1))
                pe.wait_ge(st_free, 16 * i + t + 1)
                for par in range(2):
                    last = nc.tensor.matmul(st_bank[t % 2][:, par * T:(par + 1) * T],
                                            ks[0:STACK + MAXROWS, b, h, par, :],
                                            qs[0:STACK + MAXROWS, b, 2 * h:2 * h + 2, :], start=True, stop=True)
                last.then_inc(st_full, 1)

            def weigh_values(i, g, parts=(0, 1)):
                b, hh = g // 2, g % 2
                bank = o_bank[g % 2]
                if 0 in parts:
                    pe.wait_ge(st_free, 16 * i + 4 * g + 4 + 2)
                    pe.wait_ge(o_free, 4 * i + g + 1)
                for what in parts:
                    for par in range(2):
                        for j in range(4):
                            lo = HD * (1 - par)
                            w = vpad[:, b, 4 * hh + j, lo:lo + 2 * HD] if what == 0 else onepad[:, lo:lo + 2 * HD]
                            last = nc.tensor.matmul(bank[32 * j:32 * j + 32, what * T:(what + 1) * T], w,
                                                    probs[:, g % 2, j, par, :], start=(par == 0), stop=(par == 1),
                                                    tile_position=(0, 32 * j))
                if 1 in parts: last.then_inc(weighed, 1)

            def project_out(i, b, F):
                f = claim(f"o{b}", F) if b == 0 or F is fill_last else F("o1")
                pe.wait_ge(oT_lo, 4 * i + 2 * b + 2)
                three(g_bank[f.bank][:, :], lambda a, k: oT[:, a, k, b * SEQ:(b + 1) * SEQ],
                      lambda c, k: wo[:, c, k, :], KT).then_inc(g_full[f.bank], 1)

            pe.wait_ge(ident_ready, 1)
            keep_warm(WARM_START)
            for b in range(2):
                pe.wait_ge(xn_ready, b + 1)
                transposed(f"xT{b}", fill_first, xn[:, b, :])
            keep_warm(WARM_SPLIT)
            pe.wait_ge(ctx_in, 16)
            transposed("cT0", fill_first, ctxb[:, 0, :])
            ready("xT0", fill_first)
            ready("xT1", fill_first)
            pe.wait_ge(wq_lo, KT)
            claim("q0", fill_first)
            project_q_tile(0, fill_first)
            project_q_tile(1, fill_first)
            transposed("cT1", fill_first, ctxb[:, 1, :])
            keep_warm(WARM_SPLIT // 2)
            ready("cT0", fill_first)
            ready("cT1", fill_first)
            pe.wait_ge(wkv_lo, 2)
            project_k(fill_first)
            claim("q1", fill_first)
            project_q_tile(2, fill_first)
            project_q_tile(3, fill_first)
            project_v(fill_first)
            pe.wait_ge(consts, 1)
            keep_warm(WARM_STACK)
            for s in range(8):
                scores(0, s)
                keep_warm(1)
            transpose_max(0, 0, fill_first)
            keep_warm(WARM_MAX)
            pe.wait_ge(pool_const, 4)
            for t in range(4):
                scores_t(0, t)
                scores(0, 8 + t)
            with pe.Fori(0, PAIRS - 1) as i:
                def F(name):
                    return fill_body(name, i)
                for t in range(4, 8):
                    scores_t(i, t)
                    scores(i, 8 + t)
                    if t == 4:
                        pe.wait_ge(ctx_in, 16 * i + 32)
                        transposed("cT0", F, ctxb[:, 0, :])
                    if t == 5:
                        transposed("cT1", F, ctxb[:, 1, :])
                        weigh_values(i, 0, (0,))
                    if t == 6:
                        weigh_values(i, 0, (1,))
                        pe.wait_ge(xn_ready, 2 * i + 3)
                        transposed("xT0", F, xn[:, 0, :])
                    if t == 7:
                        pe.wait_ge(xn_ready, 2 * i + 4)
                        transposed("xT1", F, xn[:, 1, :])
                ready("cT0", F)
                ready("cT1", F)
                project_k(F)
                ready("xT0", F)
                ready("xT1", F)
                claim("q0", F)
                project_q_tile(0, F)
                project_q_tile(1, F)
                transpose_max(i, 1, F)
                weigh_values(i, 1)
                claim("q1", F)
                project_q_tile(2, F)
                scores_t(i, 8)
                scores_t(i, 9)
                project_q_tile(3, F)
                for t in range(10, 16):
                    scores_t(i, t)
                    if t == 11:
                        pe.wait_ge(wo_lo, 1)
                        project_out(i, 0, F)
                        weigh_values(i, 2)
                    if t >= 12: scores(i + 1, t - 12)
                for s in range(4, 8):
                    scores(i + 1, s)
                    if s == 5: weigh_values(i, 3, (0,))
                weigh_values(i, 3, (1,))
                transpose_max(i + 1, 0, F)
                project_v(F)
                f = claim("o1", F)
                keep_warm(WARM_LOOP, g_bank[f.bank])
                for t in range(4):
                    scores_t(i + 1, t)
                    if t == 1: scores(i + 1, 8)
                    if t == 2: scores(i + 1, 9)
                project_out(i, 1, F)
                scores(i + 1, 10)
                scores(i + 1, 11)
            last_pair = PAIRS - 1

            def transpose_x2(i, b):
                pe.wait_ge(x2n_ready, 2 * i + b + 1)
                for k in range(KT):
                    last = nc.tensor.transpose(x2_bank(i, b)[:, k, :], xn[:, b, k * P:(k + 1) * P], ident[:, :])
                last.then_inc(x2_full, 1)

            for t in range(4, 8):
                scores_t(last_pair, t)
                scores(last_pair, 8 + t)
                if t == 4:
                    f = claim("eT", fill_last)
                    pe.wait_ge(small_in, 48)
                    for m in range(LT):
                        for l in range(LT):
                            last = nc.tensor.transpose(g_bank[f.bank][:, (2 * m + l) * P:(2 * m + l + 1) * P],
                                                       raw2[:, l * LAT + m * P:l * LAT + (m + 1) * P], ident[:, :])
                    last.then_inc(g_full[f.bank], 1)
                if t == 5: weigh_values(last_pair, 0, (0,))
                if t == 6: weigh_values(last_pair, 0, (1,))
            transpose_max(last_pair, 1, fill_last)
            weigh_values(last_pair, 1)
            ready("eT", fill_last)

            def fold_experts(l):
                f = claim(f"ef{l}", fill_last)
                for m in range(LT):
                    last = nc.tensor.matmul(g_bank[f.bank][:, :], expT[:, m, l * P:(l + 1) * P],
                                            raw2[:, 512 + m * D:512 + (m + 1) * D],
                                            start=(m == 0), stop=(m == LT - 1))
                last.then_inc(g_full[f.bank], 1)

            fold_experts(0)
            scores_t(last_pair, 8)
            scores_t(last_pair, 9)
            pe.wait_ge(s_free, 16 * PAIRS + 2)
            for b in range(2):
                transpose_x2(0, b)
            scores_t(last_pair, 10)
            scores_t(last_pair, 11)
            fold_experts(1)
            for t in range(12, 16):
                scores_t(last_pair, t)
            weigh_values(last_pair, 2)
            weigh_values(last_pair, 3)
            for b in range(2):
                project_out(last_pair, b, fill_last)
            pe.wait_ge(o_free, 4 * PAIRS + 2)
            pe.wait_ge(up_lo, KT)
            ready("ef0", fill_last)
            ready("ef1", fill_last)

            def ffn(i, more):
                pe.wait_ge(x2_lo, 2 * i + 2)
                for u in range(MT // 2):
                    pe.wait_ge(up_free, 4 * i + u + 1)
                    for m in range(2):
                        cols = (2 * u + m) * P
                        last = three(s_bank[u % 2][:, m * T:(m + 1) * T], lambda a, k: up[:, a, k, cols:cols + P],
                                     lambda c, k: x2T[:, c, k, :], KT)
                    last.then_inc(up_full, 1)
                pe.wait_ge(fc1_lo, 1)
                pe.wait_ge(small_lo, 1)
                pe.wait_ge(routed_scaled, 2 * i + 2)
                for m in range(LT):
                    last = three(o_bank[0][:, m * T:(m + 1) * T], lambda a, k: fc1[:, a, k, m * P:(m + 1) * P],
                                 lambda c, k: x2T[:, c, k, :], KT)
                last.then_inc(lat_full, 1)
                for b in range(2):
                    at = 2 * NE * b
                    for k in range(KT):
                        nc.tensor.matmul(o_bank[1][:, at:at + 2 * NE], x2T[:, 0, k, b * SEQ:(b + 1) * SEQ],
                                         gw[:, k, :, :], start=(k == 0), stop=False)
                    for k in range(KT):
                        last = nc.tensor.matmul(o_bank[1][:, at:at + NE], x2T[:, 1, k, b * SEQ:(b + 1) * SEQ],
                                                gw[:, k, 0, :], start=False, stop=(k == KT - 1))
                last.then_inc(logits_full, 1)
                if more:
                    for b in range(2):
                        transpose_x2(i + 1, b)
                pe.wait_ge(down_lo, MT)
                pe.wait_ge(h_lo, 4 * i + 4 + 2)
                def down_product(b):
                    pe.wait_ge(y_ready, 2 * i + b + 1)
                    three(g_bank[b][:, :], lambda a, k: hT[:, a, k, b * SEQ:(b + 1) * SEQ],
                          lambda c, k: down[:, c, k, :], MT).then_inc(down_full, 1)

                down_product(0)
                pe.wait_ge(lat_lo, i + 1)
                pe.wait_ge(rw_ready, i + 1)
                for b in range(2):
                    three(o_bank[b][:, :], lambda a, k: latT[:, a, k, b * SEQ:(b + 1) * SEQ],
                          lambda c, k: ef[:, c, k, :], LT).then_inc(routed_full, 1)
                down_product(1)

            with pe.Fori(0, PAIRS - 1) as i:
                ffn(i, True)
            ffn(PAIRS - 1, False)


_INS = ['x', 'ctx_4096', 'g_xattn', 'g_ffn', 'L0_xattn_Wq', 'L0_xattn_Wk', 'L0_xattn_Wv', 'L0_xattn_Wo',
        'L0_ffn_gate_w', 'L0_ffn_up_w', 'L0_ffn_down_w', 'L0_ffn_fc1_w', 'L0_ffn_fc2_w', 'L0_ffn_expert_w',
        'L0_ffn_ln_gamma', 'L0_ffn_ln_beta']
_OUT = ((8, 128, 512), 'float32')


def kernel(**inputs):
    import numpy as _np
    import concourse.bacc as _bacc
    from concourse.bass_utils import run_bass_kernel_spmd as _run

    nc = _bacc.Bacc("TRN2", target_bir_lowering=False, num_devices=1)
    arrays, args = {}, []
    for name in _INS:
        a = _np.ascontiguousarray(inputs[name])
        arrays[f"in_{name}_dram"] = a
        args.append(nc.dram_tensor(f"in_{name}_dram", a.shape, mybir.dt.from_np(a.dtype), kind="ExternalInput").ap())
    args.append(nc.dram_tensor("out_0_dram", _OUT[0], mybir.dt.from_np(_np.dtype(_OUT[1])), kind="ExternalOutput").ap())
    flamingo_block(nc, *args)
    r = _run(nc, [arrays], core_ids=[0])
    return r.results[0]["out_0_dram"]
```
